# Optimizing a Trainium2 kernel written in Bass

```python
import numpy as np
import jax
import jax.numpy as jnp

def _softmax(x, axis=-1):
    return jax.nn.softmax(x, axis=axis)

def _gelu(x):
    return jax.nn.gelu(x, approximate=True)

def _silu(x):
    return jax.nn.silu(x)

def _sigmoid(x):
    return jax.nn.sigmoid(x)

def _layernorm(x, axis=-1, eps=1e-05):
    m = jnp.mean(x, axis=axis, keepdims=True)
    v = jnp.var(x, axis=axis, keepdims=True)
    return (x - m) / jnp.sqrt(v + eps)

def _scatter_add(tgt, idx, src, axis=0):
    return tgt.at[idx].add(src)

def _segment_sum(src, seg, n):
    return jax.ops.segment_sum(src, seg, n)
kernel_name = 'mk_gnn_preln_d2_gnn_r32_f2011f'

def setup_inputs(seed: int=0):
    np.random.seed(seed)
    _w = jnp.asarray

    def _rec_inputs():
        import jax
        import jax.numpy as jnp
        _gk = jax.random.key(seed)
        x = -0.0003713 + 1 * jax.random.normal(jax.random.fold_in(_gk, 1), (3125, 128), jnp.float32)
        src = jax.random.randint(jax.random.fold_in(_gk, 2), (100000,), 0, 3125, jnp.int32)
        dst = jax.random.randint(jax.random.fold_in(_gk, 3), (100000,), 0, 3125, jnp.int32)
        _o = jnp.argsort(dst, stable=True)
        src = src[_o]
        dst = dst[_o]
        return (x, src, dst)
    x, src, dst = _rec_inputs()

    def _L0_gnn_setup():
        import jax, jax.numpy as jnp
        import numpy as np
        N_NODES = 3125
        N_EDGES = 50000
        D_IN, D_HID, D_OUT = (128, 256, 128)

        def _l2norm(v, eps=1e-12):
            n = jnp.linalg.norm(v, axis=-1, keepdims=True)
            return v / jnp.maximum(n, eps)

        def _priv_conv(h, src, dst, n, Wl, bl, Wr, scale):
            xn = _l2norm(h)
            agg = jax.ops.segment_sum(xn[src], dst, num_segments=n)
            h_norm = jnp.linalg.norm(h, axis=-1, keepdims=True)
            out = _l2norm(agg) * h_norm * scale
            out = out @ Wl + bl + h @ Wr
            return _l2norm(out)
        key = jax.random.key(seed)
        ks = jax.random.split(key, 8)
        x = jax.random.normal(ks[0], (N_NODES, D_IN), dtype=jnp.float32)
        edge_index = jax.random.randint(ks[1], (2, N_EDGES), 0, N_NODES, dtype=jnp.int32)
        Wl0 = jax.random.normal(ks[2], (D_IN, D_HID), dtype=jnp.float32) * 0.05
        bl0 = jnp.zeros((D_HID,), dtype=jnp.float32)
        Wr0 = jax.random.normal(ks[3], (D_IN, D_HID), dtype=jnp.float32) * 0.05
        Wl1 = jax.random.normal(ks[4], (D_HID, D_OUT), dtype=jnp.float32) * 0.05
        bl1 = jnp.zeros((D_OUT,), dtype=jnp.float32)
        Wr1 = jax.random.normal(ks[5], (D_HID, D_OUT), dtype=jnp.float32) * 0.05
        scale0 = jnp.ones((), dtype=jnp.float32)
        scale1 = jnp.ones((), dtype=jnp.float32)
        return {'x': x, 'edge_index': edge_index, 'Wl0': Wl0, 'bl0': bl0, 'Wr0': Wr0, 'Wl1': Wl1, 'bl1': bl1, 'Wr1': Wr1, 'scale0': scale0, 'scale1': scale1}
    _L0_gnn_all = _L0_gnn_setup()
    _L0_gnn_in = {k: v for k, v in _L0_gnn_all.items() if k in ('Wl0', 'bl0', 'Wr0', 'Wl1', 'bl1', 'Wr1', 'scale0', 'scale1')}
    del _L0_gnn_all

    def _L1_gnn_setup():
        import jax, jax.numpy as jnp
        import numpy as np
        N = 3125
        E = 50000
        C_IN = 128
        H = 128
        C_OUT = 128
        DEPTH = 3
        RATIO = 0.5
        EPS = 1e-05

        def gcn_conv(x, W, b, src, dst, mask, n):
            h = x @ W
            ew = mask.astype(h.dtype)
            deg = 1.0 + jax.ops.segment_sum(ew, dst, num_segments=n)
            dinv = jax.lax.rsqrt(deg)
            norm = dinv[src] * dinv[dst] * ew
            agg = jax.ops.segment_sum(h[src] * norm[:, None], dst, num_segments=n)
            agg = agg + h * (1.0 / deg)[:, None]
            return agg + b

        def bn_train(x, g, beta):
            m = jnp.mean(x, axis=0)
            v = jnp.mean((x - m) ** 2, axis=0)
            return (x - m) * jax.lax.rsqrt(v + EPS) * g + beta

        def topk_pool(x, w, src, dst, mask, k):
            score = jnp.tanh((x * w).sum(-1) / jnp.sqrt((w * w).sum()))
            _, idx = jax.lax.top_k(score, k)
            n = x.shape[0]
            new_id = jnp.zeros((n,), jnp.int32).at[idx].set(jnp.arange(k, dtype=jnp.int32))
            kept = jnp.zeros((n,), bool).at[idx].set(True)
            mask2 = mask & kept[src] & kept[dst]
            return (x[idx], new_id[src], new_id[dst], mask2, idx)
        key = jax.random.key(seed)
        ks = jax.random.split(key, 16)
        sc_in = 1.0 / np.sqrt(C_IN)
        sc_h = 1.0 / np.sqrt(H)
        sc_2h = 1.0 / np.sqrt(2 * H)
        return {'x': jax.random.normal(ks[0], (N, C_IN), jnp.float32), 'edge_index': jax.random.randint(ks[1], (2, E), 0, N, dtype=jnp.int32), 'in_W': jax.random.normal(ks[2], (C_IN, H), jnp.float32) * sc_in, 'in_b': jnp.zeros((H,), jnp.float32), 'dn_W': jax.random.normal(ks[3], (DEPTH, H, H), jnp.float32) * sc_h, 'dn_b': jnp.zeros((DEPTH, H), jnp.float32), 'dn_g': jnp.ones((DEPTH, H), jnp.float32), 'dn_beta': jnp.zeros((DEPTH, H), jnp.float32), 'pool_w': jax.random.normal(ks[4], (DEPTH, H), jnp.float32), 'bot_W': jax.random.normal(ks[5], (H, H), jnp.float32) * sc_h, 'bot_b': jnp.zeros((H,), jnp.float32), 'up_W': jax.random.normal(ks[6], (DEPTH, 2 * H, H), jnp.float32) * sc_2h, 'up_b': jnp.zeros((DEPTH, H), jnp.float32), 'up_g': jnp.ones((DEPTH, H), jnp.float32), 'up_beta': jnp.zeros((DEPTH, H), jnp.float32), 'out_W': jax.random.normal(ks[7], (H, C_OUT), jnp.float32) * sc_h, 'out_b': jnp.zeros((C_OUT,), jnp.float32)}
    _L1_gnn_all = _L1_gnn_setup()
    _L1_gnn_in = {k: v for k, v in _L1_gnn_all.items() if k in ('in_W', 'in_b', 'dn_W', 'dn_b', 'dn_g', 'dn_beta', 'pool_w', 'bot_W', 'bot_b', 'up_W', 'up_b', 'up_g', 'up_beta', 'out_W', 'out_b')}
    del _L1_gnn_all
    return {'x': x, 'src': src, 'dst': dst, 'L0_gnn_Wl0': _L0_gnn_in['Wl0'], 'L0_gnn_bl0': _L0_gnn_in['bl0'], 'L0_gnn_Wr0': _L0_gnn_in['Wr0'], 'L0_gnn_Wl1': _L0_gnn_in['Wl1'], 'L0_gnn_bl1': _L0_gnn_in['bl1'], 'L0_gnn_Wr1': _L0_gnn_in['Wr1'], 'L0_gnn_scale0': _L0_gnn_in['scale0'], 'L0_gnn_scale1': _L0_gnn_in['scale1'], 'L1_gnn_in_W': _L1_gnn_in['in_W'], 'L1_gnn_in_b': _L1_gnn_in['in_b'], 'L1_gnn_dn_W': _L1_gnn_in['dn_W'], 'L1_gnn_dn_b': _L1_gnn_in['dn_b'], 'L1_gnn_dn_g': _L1_gnn_in['dn_g'], 'L1_gnn_dn_beta': _L1_gnn_in['dn_beta'], 'L1_gnn_pool_w': _L1_gnn_in['pool_w'], 'L1_gnn_bot_W': _L1_gnn_in['bot_W'], 'L1_gnn_bot_b': _L1_gnn_in['bot_b'], 'L1_gnn_up_W': _L1_gnn_in['up_W'], 'L1_gnn_up_b': _L1_gnn_in['up_b'], 'L1_gnn_up_g': _L1_gnn_in['up_g'], 'L1_gnn_up_beta': _L1_gnn_in['up_beta'], 'L1_gnn_out_W': _L1_gnn_in['out_W'], 'L1_gnn_out_b': _L1_gnn_in['out_b']}

def reference(x, src, dst, L0_gnn_Wl0, L0_gnn_bl0, L0_gnn_Wr0, L0_gnn_Wl1, L0_gnn_bl1, L0_gnn_Wr1, L0_gnn_scale0, L0_gnn_scale1, L1_gnn_in_W, L1_gnn_in_b, L1_gnn_dn_W, L1_gnn_dn_b, L1_gnn_dn_g, L1_gnn_dn_beta, L1_gnn_pool_w, L1_gnn_bot_W, L1_gnn_bot_b, L1_gnn_up_W, L1_gnn_up_b, L1_gnn_up_g, L1_gnn_up_beta, L1_gnn_out_W, L1_gnn_out_b):
    import jax
    import jax.numpy as jnp

    def _L0_gnn_ref(x, edge_index, Wl0, bl0, Wr0, Wl1, bl1, Wr1, scale0, scale1):
        import jax, jax.numpy as jnp
        import numpy as np
        N_NODES = 3125
        N_EDGES = 50000
        D_IN, D_HID, D_OUT = (128, 256, 128)

        def _l2norm(v, eps=1e-12):
            n = jnp.linalg.norm(v, axis=-1, keepdims=True)
            return v / jnp.maximum(n, eps)

        def _priv_conv(h, src, dst, n, Wl, bl, Wr, scale):
            xn = _l2norm(h)
            agg = jax.ops.segment_sum(xn[src], dst, num_segments=n)
            h_norm = jnp.linalg.norm(h, axis=-1, keepdims=True)
            out = _l2norm(agg) * h_norm * scale
            out = out @ Wl + bl + h @ Wr
            return _l2norm(out)
        n = x.shape[0]
        loops = jnp.arange(n, dtype=edge_index.dtype)
        src = jnp.concatenate([edge_index[0], loops])
        dst = jnp.concatenate([edge_index[1], loops])
        h = _priv_conv(x, src, dst, n, Wl0, bl0, Wr0, scale0)
        h = jax.nn.relu(h)
        h = _priv_conv(h, src, dst, n, Wl1, bl1, Wr1, scale1)
        return h

    def _L1_gnn_ref(x, edge_index, in_W, in_b, dn_W, dn_b, dn_g, dn_beta, pool_w, bot_W, bot_b, up_W, up_b, up_g, up_beta, out_W, out_b):
        import jax, jax.numpy as jnp
        import numpy as np
        N = 3125
        E = 50000
        C_IN = 128
        H = 128
        C_OUT = 128
        DEPTH = 3
        RATIO = 0.5
        EPS = 1e-05

        def gcn_conv(x, W, b, src, dst, mask, n):
            h = x @ W
            ew = mask.astype(h.dtype)
            deg = 1.0 + jax.ops.segment_sum(ew, dst, num_segments=n)
            dinv = jax.lax.rsqrt(deg)
            norm = dinv[src] * dinv[dst] * ew
            agg = jax.ops.segment_sum(h[src] * norm[:, None], dst, num_segments=n)
            agg = agg + h * (1.0 / deg)[:, None]
            return agg + b

        def bn_train(x, g, beta):
            m = jnp.mean(x, axis=0)
            v = jnp.mean((x - m) ** 2, axis=0)
            return (x - m) * jax.lax.rsqrt(v + EPS) * g + beta

        def topk_pool(x, w, src, dst, mask, k):
            score = jnp.tanh((x * w).sum(-1) / jnp.sqrt((w * w).sum()))
            _, idx = jax.lax.top_k(score, k)
            n = x.shape[0]
            new_id = jnp.zeros((n,), jnp.int32).at[idx].set(jnp.arange(k, dtype=jnp.int32))
            kept = jnp.zeros((n,), bool).at[idx].set(True)
            mask2 = mask & kept[src] & kept[dst]
            return (x[idx], new_id[src], new_id[dst], mask2, idx)
        src, dst = (edge_index[0], edge_index[1])
        mask = jnp.ones((src.shape[0],), bool)
        n = x.shape[0]
        x = gcn_conv(x, in_W, in_b, src, dst, mask, n)
        xs, stack = ([], [])
        for i in range(DEPTH):
            x = gcn_conv(x, dn_W[i], dn_b[i], src, dst, mask, n)
            x = jax.nn.relu(bn_train(x, dn_g[i], dn_beta[i]))
            xs.append(x)
            k = int(RATIO * n)
            x2, src2, dst2, mask2, idx = topk_pool(x, pool_w[i], src, dst, mask, k)
            stack.append((src, dst, mask, idx, n))
            x, src, dst, mask, n = (x2, src2, dst2, mask2, k)
        x = jax.nn.relu(gcn_conv(x, bot_W, bot_b, src, dst, mask, n))
        for i in range(DEPTH):
            psrc, pdst, pmask, idx, pn = stack[DEPTH - 1 - i]
            xf = jnp.zeros((pn, x.shape[1]), x.dtype).at[idx].set(x)
            src, dst, mask, n = (psrc, pdst, pmask, pn)
            x = jnp.concatenate([xf, xs[DEPTH - 1 - i]], axis=1)
            x = gcn_conv(x, up_W[i], up_b[i], src, dst, mask, n)
            x = jax.nn.relu(bn_train(x, up_g[i], up_beta[i]))
        return gcn_conv(x, out_W, out_b, src, dst, mask, n)
    edge_index = jnp.stack([src, dst])
    h = jnp.maximum(_layernorm(x, axis=-1), 0.0)
    x = x + _L0_gnn_ref(h, edge_index, L0_gnn_Wl0, L0_gnn_bl0, L0_gnn_Wr0, L0_gnn_Wl1, L0_gnn_bl1, L0_gnn_Wr1, L0_gnn_scale0, L0_gnn_scale1)
    h = jnp.maximum(_layernorm(x, axis=-1), 0.0)
    x = x + _L1_gnn_ref(h, edge_index, L1_gnn_in_W, L1_gnn_in_b, L1_gnn_dn_W, L1_gnn_dn_b, L1_gnn_dn_g, L1_gnn_dn_beta, L1_gnn_pool_w, L1_gnn_bot_W, L1_gnn_bot_b, L1_gnn_up_W, L1_gnn_up_b, L1_gnn_up_g, L1_gnn_up_beta, L1_gnn_out_W, L1_gnn_out_b)
    return x

_drawn_inputs = setup_inputs


def setup_inputs(seed=0):
    import zlib

    import numpy as np

    out = dict(_drawn_inputs(seed))
    spreads = {'L0_gnn_bl0': (0.0, 0.525),
     'L0_gnn_bl1': (0.0, 0.1),
     'L1_gnn_in_b': (0.0, 0.1),
     'L1_gnn_dn_b': (0.0, 2.0),
     'L1_gnn_dn_g': (1.0, 0.2),
     'L1_gnn_dn_beta': (0.0, 0.1),
     'L1_gnn_bot_b': (0.0, 2.0),
     'L1_gnn_up_b': (0.0, 2.0),
     'L1_gnn_up_g': (1.0, 0.2),
     'L1_gnn_up_beta': (0.0, 0.1),
     'L1_gnn_out_b': (0.0, 0.1)}
    factors = {'L1_gnn_bot_W': 3.564}
    for name, (base, spread) in spreads.items():
        noise = np.random.default_rng([zlib.crc32(name.encode()), seed]).standard_normal(out[name].shape)
        drawn = base * np.exp(spread * noise) if base else spread * noise
        out[name] = jnp.asarray(drawn.astype(out[name].dtype))
    for name, factor in factors.items():
        out[name] = (out[name] * factor).astype(out[name].dtype)
    return out
```

```python
from contextlib import ExitStack

import concourse.bass as bass
from concourse import mybir

ALU = mybir.AluOpType
ACT = mybir.ActivationFunctionType
AX = mybir.AxisListType
F32 = mybir.dt.float32
F16 = mybir.dt.float16
BF16 = mybir.dt.bfloat16
FP8 = mybir.dt.float8e4
I32 = mybir.dt.int32
U32 = mybir.dt.uint32

P = 128
NODES, FEAT, EDGES = 3125, 128, 100000
TILES = -(-NODES // P)
TAIL = NODES - (TILES - 1) * P
PAD = TILES * P

BLOCKS = 7
BLOCK = 448
COLS = BLOCKS * BLOCK
assert NODES <= COLS <= PAD

WIN = 8
WINDOWS = COLS // WIN
SLOTS = 384
CHUNKS = SLOTS // P
GRAIN = 32
ROWS = (EDGES - SLOTS) // GRAIN + 1
GROUPS = 4
KEYS = TILES * WIN
PER_IT = 8
ITS = WINDOWS // PER_IT
RING = 4
EP, EC = 125, 800
DMA = 16

LEVEL_NODES = (NODES, NODES // 2, NODES // 4, NODES // 8)
CONVS = (("in", 0, 0, 1, None), ("dn", 0, 1, 1, 0), ("dn", 1, 2, 1, 1), ("dn", 2, 3, 1, 2), ("bot", 3, 4, 1, None),
         ("up", 2, 5, 2, 0), ("up", 1, 7, 2, 1), ("up", 0, 9, 2, 2), ("out", 0, 11, 1, None))
W_SLOTS = 12
POOLED = (2, 3, 4)
UNSCALED = (1, 5)
FIRST_UNIT = 3
V_IN_B, V_DN_B, V_DN_G, V_DN_BETA, V_POOL, V_BOT_B, V_UP_B, V_UP_G, V_UP_BETA, V_OUT_B = 0, 1, 4, 7, 10, 13, 14, 17, 20, 23
V_ROWS = 24
UNIT_SCALE = 8192.0
RSQRT_MAGIC = 1597463007.0
GROUPS4 = [(t, min(4, TILES - t)) for t in range(0, TILES, 4)]
GROUPS2 = [(t, min(2, TILES - t)) for t in range(0, TILES, 2)]
TANH_CLAMP = 7.90531110763549805
TANH_P = (-2.76076847742355e-16, 2.00018790482477e-13, -8.60467152213735e-11, 5.12229709037114e-08,
          1.48572235717979e-05, 6.37261928875436e-04, 4.89352455891786e-03)
TANH_Q = (1.19825839466702e-06, 1.18534705686654e-04, 2.26843463243900e-03, 4.89352518554385e-03)
FAN = 16


def key_steps(level):
    return [(2 * lv + half, (4096, 256, 16, 1)) for lv in range(level, -1, -1) for half in range(2)] + [(6, (256, 16, 1))]


def gnn_kernel(nc, a, out):
    with ExitStack() as ctx:
        def sb(name, shape, dt):
            return ctx.enter_context(nc.sbuf_tensor(name, shape, dt))

        def sem(name):
            return ctx.enter_context(nc.semaphore(name))

        def dram(name, shape, dt):
            return nc.dram_tensor(name, shape, dt, kind="Internal").ap()

        last_row = dram("last_row", (EDGES // GRAIN,), F32)
        src_table = dram("src_table", (ROWS, SLOTS), I32)
        dst_table = dram("dst_table", (ROWS, SLOTS), I32)

        dk_dram = dram("dk_dram", (4, 2 * TILES, P), F32)
        xs_dram = dram("xs_dram", (3, P, PAD), F32)

        adj = sb("adj", [P, TILES * PAD], FP8)
        region1 = sb("region1", [P, 6400], F32)
        region2 = sb("region2", [P, 6400], F32)
        region3 = sb("region3", [P, 6400], F32)
        ident = sb("ident", [P, P], F32)
        iota_lo = sb("iota_lo", [P, P], BF16)
        iota_key = sb("iota_key", [P, KEYS], BF16)
        win_base = sb("win_base", [P, GROUPS], F32)
        scalars = sb("scalars", [P, 2, CHUNKS, PER_IT], F32)
        row_f = sb("row_f", [P, GROUPS], F32)
        row_i = sb("row_i", [P, GROUPS], U32)
        uncovered = sb("uncovered", [P, GROUPS], F32)
        minus15 = sb("minus15", [P, 1], F32)
        excess = sb("excess", [P, WINDOWS // 2], F32)

        parts = sb("parts", [P, 6400], F32)
        nodebuf = sb("nodebuf", [P, PAD], F32)
        weights = sb("weights", [P, W_SLOTS, P], F32)
        scales = sb("scales", [P, 2], F32)
        vec_rows = sb("vec_rows", [V_ROWS, P], F32)
        vecs = sb("vecs", [P, V_ROWS], F32)
        ones = sb("ones", [P, P], F32)
        bounds = sb("bounds", [P, W_SLOTS], F32)
        fit = sb("fit", [P, 9], F32)
        unfit = sb("unfit", [P, 9], F32)
        bn = sb("bn", [P, 8], F32)
        tiny = sb("tiny", [P, 12, TILES], F32)
        dcol = sb("dcol", [P, 4, 2, TILES], F32)
        kept16 = sb("kept16", [P, TILES], BF16)
        keys = sb("keys", [P, 7, TILES], F32)
        pool_norm = sb("pool_norm", [P, 3], F32)
        steps_iota = sb("steps_iota", [P, 4, FAN], F32)
        search = sb("search", [P, 64], F32)
        compare_buf = parts[:, 3200:3200 + FAN * TILES].rearrange("p (j t) -> p j t", j=FAN)
        key_work = parts[:, 3700:3700 + 8 * TILES].rearrange("p (k t) -> p k t", k=8)
        dk_rows = parts[0:2 * TILES, 4000:4000 + P]

        def tiles(ap):
            return ap.rearrange("p (t f) -> p t f", t=TILES)

        def per_node(col, n=FEAT):
            return col.rearrange("p (t o) -> p t o", o=1).broadcast_to((P, TILES, n))

        wl0, wr0, bias0 = (region3[:, 3600 + 256 * k:3856 + 256 * k] for k in range(3))
        wl1, wr1 = (region3[:, 4368 + 256 * k:4624 + 256 * k].rearrange("p (m f) -> p m f", m=2) for k in range(2))
        bias1 = region3[:, 4880:5008]
        h0t, agg0t = region2[:, 0:PAD], region2[:, PAD:2 * PAD]
        parts0 = parts[:, 0:3200].bitcast(F16).rearrange("p (t k f) -> p t k f", t=TILES, k=2)
        parts1 = parts[:, :].bitcast(F16).rearrange("p (t k f) -> p t k f", t=TILES, k=2)
        squares = parts[:, 3200:6400]
        out0 = region1[:, :].rearrange("p (t f) -> p t f", t=TILES)
        h1t = region2[:, :].rearrange("p (m n) -> p m n", m=2)
        agg1t = region1[:, :].rearrange("p (m n) -> p m n", m=2)
        squares1 = parts[:, :].rearrange("p (m n) -> p m n", m=2)
        junk0 = parts[:, 3200:6400].bitcast(BF16).rearrange("p (t f) -> p t f", t=TILES)
        junk1 = region3[:, 0:3200].bitcast(BF16).rearrange("p (t f) -> p t f", t=TILES)
        junk2 = parts[:, 0:1600].bitcast(BF16).rearrange("p (t f) -> p t f", t=TILES)
        proj_tmp = region3[:, 6400 - 512:6400].rearrange("p (r f) -> p r f", r=2)
        out1 = region3[:, 0:PAD]
        nodes_t = region2[:, 0:PAD]
        agg_t = region2[:, PAD:2 * PAD]
        skip_t = region1[:, 0:PAD]
        d_all = region1[:, PAD:PAD + COLS]
        k_all = region3[:, 0:COLS]
        abs_w = parts[:, 3200:3200 + W_SLOTS * P].rearrange("p (s f) -> p s f", s=W_SLOTS)
        diag_fit = parts[:, 4800:4800 + P]

        dst_in = region1[0:EP, 0:EC].bitcast(I32)
        last_in = region1[0:EP, EC:EC + EC // GRAIN]
        last_all = region1[:, 1024:1024 + EDGES // GRAIN]
        compared = region2[:, 0:EDGES // GRAIN]
        edge_src = region2[:, 3200:3200 + GROUPS * SLOTS].bitcast(I32).rearrange("p (g s) -> p g s", g=GROUPS)
        edge_dst = region2[:, 4800:4800 + GROUPS * SLOTS].bitcast(I32).rearrange("p (g s) -> p g s", g=GROUPS)
        work = [region1[:, 4352 + SLOTS * k:4352 + SLOTS * (k + 1)] for k in range(4)]
        lo_rows = region2[:, 0:GROUPS * SLOTS].rearrange("p (g s) -> p g s", g=GROUPS)
        key_rows = region2[:, 1600:1600 + GROUPS * SLOTS].rearrange("p (g s) -> p g s", g=GROUPS)
        by_edge = region1[:, 0:2 * CHUNKS * 512].rearrange("p (k c w) -> p k c w", k=2, c=CHUNKS)
        hot_lo = region3[:, 0:RING * CHUNKS * 64].bitcast(BF16).rearrange("p (r c n) -> p r c n", r=RING, c=CHUNKS)
        hot_key = region3[:, 768:768 + RING * CHUNKS * 100].bitcast(BF16).rearrange("p (r c n) -> p r c n", r=RING, c=CHUNKS)
        stage = region3[:, 2048:2048 + 4 * 100].bitcast(FP8).rearrange("p (b t n) -> p b t n", b=4, t=TILES)
        stage_words = region3[:, 2048:2048 + 4 * 100].bitcast(U32).rearrange("p (b t n) -> p b t n", b=4, t=TILES)
        relu_out = region3[:, 2560:2560 + 4 * 200].bitcast(BF16).rearrange("p (b n) -> p b n", b=4)
        adj_words = adj[:, :].bitcast(U32).rearrange("p (t n) -> p t n", t=TILES)

        psum = ctx.enter_context(nc.psum_tensor("psum", [P, 8, 512], F32))

        edges_in = sem("edges_in")
        table_in = sem("table_in")
        last_picked = sem("last_picked")
        last_out = sem("last_out")
        last_back = sem("last_back")
        pool_step = sem("pool_step")
        consts_ready = sem("consts_ready")
        rows_known = sem("rows_known")
        gathered = [sem(f"gathered{g}") for g in range(GROUPS)]
        keyed = sem("keyed")
        turned = sem("turned")
        by_edge_ready = sem("by_edge_ready")
        dve_step = sem("dve_step")
        hot_ready = sem("hot_ready")
        window_done = sem("window_done")
        bank_free = sem("bank_free")
        stage_free = sem("stage_free")
        adj_placed = sem("adj_placed")
        adj_ready = sem("adj_ready")
        scalars_ready = sem("scalars_ready")

        pads_zeroed = sem("pads_zeroed")
        x_in = sem("x_in")
        weights_in = sem("weights_in")
        vec_turned = sem("vec_turned")
        abs_ready = sem("abs_ready")
        bound_ready = sem("bound_ready")
        diag_ready = sem("diag_ready")
        row_ready = sem("row_ready")
        centered = sem("centered")
        squared = sem("squared")
        h0_ready = sem("h0_ready")
        h0_squared = sem("h0_squared")
        scaled0 = sem("scaled0")
        hi0_ready = sem("hi0_ready")
        parts0_ready = sem("parts0_ready")
        h0_turned = sem("h0_turned")
        h0t_ready = sem("h0t_ready")
        kept_ready = sem("kept_ready")
        deg_ready = sem("deg_ready")
        dk_ready = sem("dk_ready")
        dk_turned = sem("dk_turned")
        dkrows_ready = sem("dkrows_ready")
        dk_out = sem("dk_out")
        db_in = sem("db_in")
        kb_in = sem("kb_in")
        agg_half = sem("agg_half")
        blocks_out = sem("blocks_out")
        agg_zeroed = sem("agg_zeroed")
        sq_ready = sem("sq_ready")
        norm_ready = sem("norm_ready")
        proj_ready = sem("proj_ready")
        proj_done = sem("proj_done")
        ss_ready = sem("ss_ready")
        h1_ready = sem("h1_ready")
        h1_squared = sem("h1_squared")
        rns_ready = sem("rns_ready")
        hi1_ready = sem("hi1_ready")
        lo1_ready = sem("lo1_ready")
        h1_turned = sem("h1_turned")
        h1t_ready = sem("h1t_ready")
        x_again = sem("x_again")
        h2_ready = sem("h2_ready")
        h2_turned = sem("h2_turned")
        h2t_ready = sem("h2t_ready")
        xt_ready = sem("xt_ready")
        score_ready = sem("score_ready")
        totals_in = sem("totals_in")
        totals_out = sem("totals_out")
        hw_ready = sem("hw_ready")
        hi_ready = sem("hi_ready")
        lo_ready = sem("lo_ready")
        v_centered = sem("v_centered")
        v_squared = sem("v_squared")
        coef_ready = sem("coef_ready")
        relu_done = sem("relu_done")
        xs_out = sem("xs_out")
        weights_fit = sem("weights_fit")
        xs_in = sem("xs_in")
        final_ready = sem("final_ready")
        final_turned = sem("final_turned")
        w2_ready = sem("w2_ready")
        stored = sem("stored")

        block = ctx.enter_context(nc.Block())

        N_WEIGHTS = 15

        def row_of(vector):
            return vector.rearrange("(o n) -> o n", o=1)

        def load_x(eng, signal):
            whole = (TILES - 1) * P
            eng.dma_start(nodebuf[:, 0:whole].rearrange("p (t f) -> p t f", f=FEAT),
                          a["x"][0:whole, :].rearrange("(t p) f -> p t f", p=P)).then_inc(signal, DMA)
            eng.dma_start(nodebuf[0:TAIL, whole:PAD], a["x"][whole:NODES, :]).then_inc(signal, DMA)

        @block.sync
        def _(sp):
            sp.dma_start(dst_in, a["dst"].rearrange("(p c) -> p c", p=EP)).then_inc(edges_in, DMA)
            for table, edges in ((src_table, a["src"]), (dst_table, a["dst"])):
                for r0, r1 in ((0, ROWS // 16 * 16), (ROWS // 16 * 16, ROWS)):
                    rows = bass.AP(edges.tensor, r0 * GRAIN, [[GRAIN, r1 - r0], [1, SLOTS]])
                    sp.dma_start(table[r0:r1, :], rows).then_inc(table_in, DMA)
            sp.wait_ge(last_picked, 1)
            sp.dma_start(last_row.rearrange("(p c) -> p c", p=EP), last_in).then_inc(last_out, DMA)
            sp.wait_ge(last_out, DMA)
            sp.dma_start(last_all, last_row.rearrange("(o c) -> o c", o=1).broadcast_to((P, EDGES // GRAIN))).then_inc(last_back, DMA)
            sp.wait_ge(parts0_ready, 1)
            sp.wait_ge(h0t_ready, len(GROUPS4))
            load_x(sp, x_again)
            loaded = 0
            for i, (kind, level, slot, slots, norm) in enumerate(CONVS):
                if i == 0 or i in POOLED:
                    sp.wait_ge(dkrows_ready, level + 1)
                    sp.dma_start(dk_dram[level], dk_rows).then_inc(dk_out, DMA)
                    sp.wait_ge(dk_out, DMA * (level + 1))
                row = dk_dram[level].rearrange("(v t) p -> v (t p)", v=2)
                if i == 0 or CONVS[i - 1][1] != level:
                    if i == 0:
                        sp.wait_ge(proj_done, 2 * TILES)
                    sp.wait_ge(blocks_out, BLOCKS * (FIRST_UNIT + i))
                    sp.dma_start(d_all, row[0:1, 0:COLS].broadcast_to((P, COLS))).then_inc(db_in, DMA)
                    if level > 0:
                        sp.wait_ge(xt_ready, i)
                        sp.dma_start(k_all, row[1:2, 0:COLS].broadcast_to((P, COLS))).then_inc(kb_in, DMA)
                if kind == "up":
                    sp.wait_ge(xs_out, DMA * 3)
                    sp.wait_ge(hw_ready, len(GROUPS4) * i)
                    sp.dma_start(skip_t, xs_dram[level]).then_inc(xs_in, DMA)
                if i in (1, 2, 3):
                    sp.wait_ge(xt_ready, i + 1)
                    sp.dma_start(xs_dram[level], nodes_t).then_inc(xs_out, DMA)
            sp.wait_ge(final_ready, len(GROUPS4))
            whole = (TILES - 1) * P
            sp.dma_start(out[0:whole, :].rearrange("(t p) f -> p t f", p=P), 
                         nodebuf[:, 0:whole].rearrange("p (t f) -> p t f", f=FEAT)).then_inc(stored, DMA)
            sp.dma_start(out[whole:NODES, :], nodebuf[0:TAIL, whole:PAD]).then_inc(stored, DMA)
            sp.wait_ge(stored, 2 * DMA)

        @block.gpsimd
        def _(pool):
            pool.memset(ident[:], 0.0).then_inc(pool_step, 1)
            pool.wait_ge(pool_step, 1)
            pool.affine_select(out=ident[:], in_=ident[:], compare_op=ALU.not_equal, fill=1.0, base=0,
                               pattern=[[-1, P]], channel_multiplier=1).then_inc(consts_ready, 1)
            pool.iota(win_base[:], pattern=[[P * WIN, GROUPS]], base=0, channel_multiplier=WIN,
                      allow_small_or_imprecise_dtypes=True).then_inc(consts_ready, 1)
            pool.iota(iota_lo[:], pattern=[[1, P]], base=0, channel_multiplier=0,
                      allow_small_or_imprecise_dtypes=True).then_inc(consts_ready, 1)
            pool.iota(iota_key[:], pattern=[[1, KEYS]], base=0, channel_multiplier=0,
                      allow_small_or_imprecise_dtypes=True).then_inc(consts_ready, 1)
            pool.memset(minus15[:], -15.0).then_inc(consts_ready, 1)
            pool.memset(ones[:], 1.0).then_inc(consts_ready, 1)
            for n, step in enumerate((4096, 256, 16, 1)):
                pool.iota(steps_iota[:, n, :], pattern=[[step, FAN]], base=0, channel_multiplier=0,
                          allow_small_or_imprecise_dtypes=True).then_inc(consts_ready, 1)
            pool.iota(keys[:, 6, :], pattern=[[-P, TILES]], base=4095, channel_multiplier=-1,
                      allow_small_or_imprecise_dtypes=True).then_inc(consts_ready, 1)
            pool.memset(adj_words[:, :, COLS // 4:PAD // 4], 0).then_inc(adj_placed, 1)
            pool.wait_ge(rows_known, 1)
            pool.wait_ge(table_in, 4 * DMA)
            for g in range(GROUPS):
                for rows, table in ((edge_src, src_table), (edge_dst, dst_table)):
                    pool.indirect_dma_start(out=rows[:, g, :], out_offset=None, in_=table,
                                            in_offset=bass.IndirectOffsetOnAxis(ap=row_i[:, g:g + 1], axis=0)
                                            ).then_inc(gathered[g], DMA)
            pool.sem_inc(stage_free, 4)
            with pool.Fori(0, ITS) as it:
                for b in range(4):
                    pool.wait_ge(bank_free, 4 * it + (4 + b + 1))
                    pool.tensor_copy(adj_words[:, :, bass.ds(16 * it + 4 * b, 4)], stage_words[:, b]).then_inc(stage_free, 1)

        @block.vector
        def _(dve):
            steps = [0]

            def step(ins):
                ins.then_inc(dve_step, 1)
                steps[0] += 1
                dve.wait_ge(dve_step, steps[0])

            def rsqrt(to, of, half):
                v = nc.vector
                step(v.tensor_scalar(half.bitcast(I32), of.bitcast(I32), 1, None, ALU.logical_shift_right))
                step(v.tensor_scalar(to.bitcast(I32), half.bitcast(I32), -1.0, RSQRT_MAGIC, ALU.mult, ALU.add))
                for _ in range(4):
                    step(v.tensor_tensor(half, to, to, ALU.mult))
                    step(v.scalar_tensor_tensor(half, half, -0.5, of, ALU.mult, ALU.mult))
                    step(v.scalar_tensor_tensor(to, half, 1.5, to, ALU.add, ALU.mult))

            def inverse_norms(inv, norm, squares_sum):
                half = tiny[:, 11, :]
                step(nc.vector.tensor_scalar(norm, squares_sum, 1e-30, None, ALU.max))
                rsqrt(inv, norm, half)
                step(nc.vector.tensor_scalar(inv, inv, 1e12, None, ALU.min))
                step(nc.vector.tensor_tensor(norm, squares_sum, inv, ALU.mult))

            def layernorm(src, to, junk, n):
                total, inv = tiny[:, 0, :], tiny[:, 1, :]
                step(nc.vector.tensor_reduce(total, tiles(src), AX.X, ALU.add))
                step(nc.vector.tensor_scalar(total, total, -1.0 / FEAT, None, ALU.mult))
                nc.vector.tensor_tensor(tiles(src), tiles(src), per_node(total), ALU.add).then_inc(centered, 1)
                dve.wait_ge(centered, n)
                dve.wait_ge(squared, n)
                step(nc.vector.tensor_reduce(total, tiles(junk), AX.X, ALU.add))
                step(nc.vector.tensor_scalar(total, total, 1.0 / FEAT, 1e-5, ALU.mult, ALU.add))
                rsqrt(inv, total, tiny[:, 11, :])
                return nc.vector.scalar_tensor_tensor(tiles(to), tiles(src), 0.0, per_node(inv), ALU.max, ALU.mult)

            def fit_powers(c0, c1, psum_cols):
                bits = bn[:, 0:1] if c1 - c0 == 1 else tiny[:, 10, 0:c1 - c0]
                f, u = fit[:, c0:c1], unfit[:, c0:c1]
                step(nc.vector.tensor_scalar(bits, psum_cols, 2.0 ** -100, None, ALU.max))
                step(nc.vector.tensor_scalar(bits.bitcast(I32), bits.bitcast(I32), 0x7F800000, None, ALU.bitwise_and))
                step(nc.vector.tensor_scalar(f.bitcast(I32), bits.bitcast(I32), -1.0, float(268 << 23), ALU.mult, ALU.add))
                step(nc.vector.tensor_scalar(u.bitcast(I32), f.bitcast(I32), -1.0, float(254 << 23), ALU.mult, ALU.add))

            fitted = [0]

            def fit_weights(i):
                _, _, slot, slots, _ = CONVS[i]
                fitted[0] += 1
                nc.vector.tensor_scalar(diag_fit, ident[:], fit[:, i:i + 1], None, ALU.mult).then_inc(diag_ready, 1)
                dve.wait_ge(row_ready, fitted[0])
                w = weights[:, slot:slot + slots, :]
                row = psum[:, 7:8, 0:P].broadcast_to((P, slots, P))
                nc.vector.tensor_tensor(w, w, row, ALU.mult).then_inc(weights_fit, 1)
                dve.wait_ge(weights_fit, fitted[0])

            dve.wait_ge(edges_in, DMA)
            nc.vector.tensor_copy(last_in, dst_in.rearrange("p (c k) -> p c k", k=GRAIN)[:, :, GRAIN - 1]).then_inc(last_picked, 1)
            nc.vector.memset(nodebuf[:, PAD - P:PAD], 0.0).then_inc(pads_zeroed, 1)
            dve.wait_ge(consts_ready, 11)
            dve.wait_ge(x_in, 2 * DMA)
            layernorm(nodebuf[:], nodebuf[:], region3[:, 0:PAD], 1).then_inc(h0_ready, 1)
            dve.wait_ge(h0_squared, 1)
            step(nc.vector.tensor_reduce(tiny[:, 2, :], tiles(region3[:, 0:PAD]), AX.X, ALU.add))
            norm0 = tiny[:, 3, :]
            inverse_norms(tiny[:, 4, :], norm0, tiny[:, 2, :])
            step(nc.vector.tensor_scalar(tiny[:, 4, :], tiny[:, 4, :], UNIT_SCALE, None, ALU.mult))
            nc.vector.tensor_tensor(tiles(region3[:, PAD:2 * PAD]), tiles(nodebuf[:]), per_node(tiny[:, 4, :]), ALU.mult).then_inc(scaled0, 1)
            dve.wait_ge(vec_turned, 1)
            step(nc.vector.tensor_copy(vecs[:], psum[:, 7, 0:V_ROWS]))
            step(nc.vector.tensor_tensor(search[:, 0:3], vecs[:, V_POOL:V_POOL + 3], vecs[:, V_POOL:V_POOL + 3], ALU.mult))
            magnitude = search[:, 16:16 + V_ROWS]
            step(nc.vector.tensor_scalar(magnitude.bitcast(I32), vecs[:].bitcast(I32), 0x7FFFFFFF, None, ALU.bitwise_and))
            step(nc.vector.memset(bounds[:], 1.0))
            step(nc.vector.memset(bounds[:, 0:1], 11.4))
            for slot, g, beta in [(2 + k, V_DN_G + k, V_DN_BETA + k) for k in range(3)] + \
                                 [(6 + 2 * k, V_DN_G + 2 - k, V_DN_BETA + 2 - k) for k in range(3)] + \
                                 [(7 + 2 * k, V_UP_G + k, V_UP_BETA + k) for k in range(2)] + [(11, V_UP_G + 2, V_UP_BETA + 2)]:
                step(nc.vector.scalar_tensor_tensor(bounds[:, slot:slot + 1], magnitude[:, g:g + 1], 56.0, magnitude[:, beta:beta + 1],
                                                    ALU.mult, ALU.add))
            dve.wait_ge(weights_in, N_WEIGHTS * DMA)
            nc.vector.tensor_scalar(abs_w.bitcast(I32), weights[:].bitcast(I32), 0x7FFFFFFF, None, ALU.bitwise_and).then_inc(abs_ready, 1)
            dve.wait_ge(bound_ready, 1)
            step(nc.vector.tensor_scalar(pool_norm[:], psum[:, 7, 32:35], 1e-30, None, ALU.max))
            step(nc.vector.tensor_copy(search[:, 4:7], pool_norm[:]))
            rsqrt(pool_norm[:], search[:, 4:7], search[:, 8:11])
            fit_powers(0, 9, psum[:, 7, 16:25])
            for i in range(len(CONVS)):
                if i not in UNSCALED:
                    fit_weights(i)
            dve.wait_ge(hi0_ready, 1)
            nc.vector.tensor_tensor(parts0[:, :, 1, :], tiles(region3[:, PAD:2 * PAD]), parts0[:, :, 0, :], ALU.subtract).then_inc(parts0_ready, 1)
            dve.wait_ge(parts0_ready, 1)
            dve.wait_ge(last_back, DMA)
            for g in range(GROUPS):
                step(nc.vector.tensor_scalar(compared, last_all, win_base[:, g:g + 1], 0.0, ALU.is_lt, ALU.add,
                                             accum_out=row_f[:, g:g + 1]))
            nc.vector.tensor_scalar(row_i[:], row_f[:], float(ROWS - 1), None, ALU.min).then_inc(rows_known, 1)
            for g in range(GROUPS):
                dve.wait_ge(gathered[g], 2 * DMA)
                low, high = work[0].bitcast(I32), work[1].bitcast(I32)
                late, outside = work[2], work[3]
                loc = key_rows[:, g, :]
                nc.vector.tensor_scalar(low, edge_src[:, g, :], P - 1, None, ALU.bitwise_and)
                nc.vector.tensor_scalar(high, edge_src[:, g, :], 7, 3, ALU.logical_shift_right, ALU.logical_shift_left)
                step(nc.vector.tensor_scalar(loc, edge_dst[:, g, :], win_base[:, g:g + 1], None, ALU.subtract))
                nc.vector.tensor_copy(lo_rows[:, g, :], low)
                step(nc.vector.tensor_scalar(late, loc, float(WIN), None, ALU.is_ge))
                step(nc.vector.scalar_tensor_tensor(outside, loc, 0.0, late, ALU.is_lt, ALU.max,
                                                    accum_out=uncovered[:, g:g + 1]))
                step(nc.vector.tensor_tensor(loc, loc, high, ALU.add))
                nc.vector.scalar_tensor_tensor(loc, outside, 4096.0, loc, ALU.mult, ALU.add).then_inc(keyed, 1)
            dve.wait_ge(by_edge_ready, 2 * GROUPS)
            dve.sem_inc(hot_ready, 1)
            with dve.Fori(0, ITS) as it:
                dve.wait_ge(hot_ready, 8 * it + 1)
                nc.vector.tensor_copy(scalars[:], by_edge[:, :, :, bass.ds(8 * it, 8)]).then_inc(scalars_ready, 1)
                dve.wait_ge(scalars_ready, it + 1)
                for w in range(PER_IT):
                    dve.wait_ge(window_done, 8 * it + (w + 1))
                    for c in range(CHUNKS):
                        nc.vector.tensor_scalar(hot_lo[:, w % RING, c, :], iota_lo[:], scalars[:, 0, c, w:w + 1], None, ALU.is_equal)
                        last = nc.vector.tensor_scalar(hot_key[:, w % RING, c, :], iota_key[:], scalars[:, 1, c, w:w + 1], None, ALU.is_equal)
                    last.then_inc(hot_ready, 1)

            dve.wait_ge(stage_free, 4 + 4 * ITS)
            for t in range(0, TILES, TILES - 1):
                n = TILES - 1 if t == 0 else 1
                o = t * (PAD + P)
                if t == 0:
                    diag = adj[:, 0:n * (PAD + P)].rearrange("p (t n) -> p t n", t=n)[:, :, 0:P]
                    one = ident[:, :].rearrange("p (o n) -> p o n", o=1).broadcast_to((P, n, P))
                else:
                    diag, one = adj[:, o:o + P], ident[:]
                nc.vector.tensor_tensor(diag, diag, one, ALU.add, saturate=False).then_inc(adj_ready, 1)

            def degrees(level):
                dve.wait_ge(deg_ready, level + 1)
                d, kept, half, deg = dcol[:, level, 0, :], dcol[:, level, 1, :], tiny[:, 11, :], tiny[:, 10, :]
                step(nc.vector.tensor_scalar(deg, psum[:, 7, 0:TILES], 1.0, None, ALU.max))
                rsqrt(d, deg, half)
                nc.vector.tensor_tensor(d, d, kept, ALU.mult).then_inc(dk_ready, 1)
                dve.wait_ge(dk_ready, level + 1)
                dve.wait_ge(dk_turned, level + 1)
                if level > 0:
                    dve.wait_ge(dk_out, DMA * level)
                nc.vector.tensor_copy(dk_rows, psum[0:2 * TILES, 7, P:2 * P]).then_inc(dkrows_ready, 1)
                dve.wait_ge(dkrows_ready, level + 1)

            def blocks_of(unit, b0, b1, take):
                for b in range(b0, b1):
                    if b in (0, 4):
                        dve.wait_ge(agg_half, 2 * unit + (1 if b == 0 else 2))
                    take(b).then_inc(blocks_out, 1)

            def first_agg(to):
                return lambda b: nc.vector.tensor_scalar(to[:, b * BLOCK:(b + 1) * BLOCK], psum[:, b, 0:BLOCK],
                                                         1.0 / UNIT_SCALE, None, ALU.mult)

            def project(layer, n, width, bias, factor, to):
                for t in range(TILES):
                    m = layer * TILES + t
                    dve.wait_ge(proj_ready, m + 1)
                    tmp = proj_tmp[:, t % 2, 0:width]
                    step(nc.vector.tensor_tensor(tmp, psum[:, t % 4, 256:256 + width], bias[:], ALU.add))
                    nc.vector.scalar_tensor_tensor(to[:, t, :], psum[:, t % 4, 0:width], factor[:, t:t + 1], tmp,
                                                   ALU.mult, ALU.add).then_inc(proj_done, 1)

            def agg_factor(layer, norm):
                dve.wait_ge(norm_ready, layer + 1)
                factor, other, total = tiny[:, 5, :], tiny[:, 6, :], tiny[:, 7, :]
                step(nc.vector.tensor_copy(total, psum[:, 7, 0:TILES]))
                inverse_norms(factor, other, total)
                step(nc.vector.tensor_scalar(factor, factor, scales[:, layer:layer + 1], None, ALU.mult))
                step(nc.vector.tensor_tensor(factor, factor, norm, ALU.mult))
                return factor

            step(nc.vector.memset(dcol[:, 0, 1, :], 1.0))
            step(nc.vector.memset(dcol[:, 0, 1, TILES - 1:TILES], 0.0))
            step(nc.vector.memset(dcol[0:TAIL, 0, 1, TILES - 1:TILES], 1.0))
            nc.vector.tensor_copy(kept16[:], dcol[:, 0, 1, :]).then_inc(kept_ready, 1)
            dve.wait_ge(kept_ready, 1)
            nc.vector.memset(agg0t[:, COLS:PAD], 0.0).then_inc(agg_zeroed, 1)
            blocks_of(0, 0, BLOCKS, first_agg(agg0t))
            dve.wait_ge(w2_ready, 8 * DMA)
            factor = agg_factor(0, norm0)
            project(0, 0, 256, bias0, factor, out0)
            dve.wait_ge(ss_ready, 1)
            inverse_norms(tiny[:, 5, :], tiny[:, 6, :], tiny[:, 8, :])
            nc.vector.scalar_tensor_tensor(out0, out0, 0.0, per_node(tiny[:, 5, :], 256), ALU.max, ALU.mult).then_inc(h1_ready, 1)
            dve.wait_ge(h1_squared, 1)
            norm1 = tiny[:, 3, :]
            inverse_norms(tiny[:, 4, :], norm1, tiny[:, 8, :])
            nc.vector.tensor_scalar(tiny[:, 4, :], tiny[:, 4, :], UNIT_SCALE, None, ALU.mult).then_inc(rns_ready, 1)
            dve.wait_ge(rns_ready, 1)
            for t in range(TILES):
                dve.wait_ge(hi1_ready, t + 1)
                nc.vector.scalar_tensor_tensor(parts1[:, t, 1, :], out0[:, t, :], tiny[:, 4, t:t + 1], parts1[:, t, 0, :],
                                               ALU.mult, ALU.subtract).then_inc(lo1_ready, 1)
            dve.wait_ge(h1t_ready, len(GROUPS2))
            dve.wait_ge(lo1_ready, TILES)
            for m in range(2):
                nc.vector.memset(agg1t[:, m, COLS:PAD], 0.0).then_inc(agg_zeroed, 1)
            for m in range(2):
                blocks_of(1 + m, 0, BLOCKS, first_agg(agg1t[:, m, :]))
            factor = agg_factor(1, norm1)
            project(1, 0, P, bias1, factor, tiles(out1))
            dve.wait_ge(ss_ready, 2)
            inverse_norms(tiny[:, 5, :], tiny[:, 6, :], tiny[:, 8, :])
            step(nc.vector.tensor_tensor(tiles(out1), tiles(out1), per_node(tiny[:, 5, :]), ALU.mult))
            dve.wait_ge(x_again, 2 * DMA)
            step(nc.vector.tensor_tensor(nodebuf[:], nodebuf[:], out1, ALU.add))
            step(nc.vector.tensor_copy(out1, nodebuf[:]))
            layernorm(out1, out1, region1[:, 0:PAD], 2).then_inc(h2_ready, 1)
            dve.wait_ge(h2_ready, 1)
            degrees(0)
            dve.wait_ge(h2t_ready, len(GROUPS4))

            vec = lambda k: vecs[:, k:k + 1]
            totals = [0]

            def total_of(n):
                totals[0] += 1
                dve.wait_ge(totals_out, totals[0])

            def tanh(to, x, p, x2):
                v = nc.vector
                step(v.tensor_scalar(x, x, TANH_CLAMP, -TANH_CLAMP, ALU.min, ALU.max))
                step(v.tensor_tensor(x2, x, x, ALU.mult))
                step(v.tensor_scalar(p, x2, TANH_P[0], TANH_P[1], ALU.mult, ALU.add))
                for c in TANH_P[2:]:
                    step(v.tensor_tensor(p, p, x2, ALU.mult))
                    step(v.tensor_scalar(p, p, c, None, ALU.add))
                step(v.tensor_tensor(p, p, x, ALU.mult))
                step(v.tensor_scalar(to, x2, TANH_Q[0], TANH_Q[1], ALU.mult, ALU.add))
                for c in TANH_Q[2:]:
                    step(v.tensor_tensor(to, to, x2, ALU.mult))
                    step(v.tensor_scalar(to, to, c, None, ALU.add))
                step(v.reciprocal(x2, to))
                step(v.tensor_tensor(to, p, x2, ALU.mult))

            def choose(level):
                v = nc.vector
                kept, chosen = dcol[:, level, 1, :], dcol[:, level + 1, 1, :]
                x, p, x2, th = (tiny[:, k, :] for k in range(5, 9))
                dve.wait_ge(score_ready, level + 1)
                step(v.tensor_scalar(x, psum[:, 7, 0:TILES], pool_norm[:, level:level + 1], None, ALU.mult))
                tanh(th, x, p, x2)
                step(v.tensor_scalar(th, th, 0.0, None, ALU.add))
                sign, bits = p.bitcast(I32), th.bitcast(I32)
                step(v.tensor_scalar(sign, bits, 31, 0x7FFFFFFF, ALU.arith_shift_right, ALU.bitwise_and))
                step(v.tensor_tensor(bits, bits, sign, ALU.bitwise_xor))
                step(v.tensor_scalar(sign, bits, 16, None, ALU.arith_shift_right))
                step(v.tensor_scalar(keys[:, 2 * level, :], sign, 32769.0, None, ALU.add))
                step(v.tensor_scalar(sign, bits, 0xFFFF, None, ALU.bitwise_and))
                step(v.tensor_scalar(keys[:, 2 * level + 1, :], sign, 1.0, None, ALU.add))
                equal, key, above = key_work[:, 0, :], key_work[:, 1, :], key_work[:, 2, :]
                base, need, count = search[:, 0:1], search[:, 1:2], search[:, 2:3]
                step(v.tensor_copy(equal, kept))
                step(v.memset(chosen, 0.0))
                step(v.memset(need, float(LEVEL_NODES[level + 1])))
                for which, steps in key_steps(level):
                    step(v.tensor_tensor(key, keys[:, which, :], equal, ALU.mult))
                    step(v.memset(base, 1.0))
                    for n, size in enumerate(steps):
                        first = n + 4 - len(steps)
                        tried = search[:, 32:32 + FAN]
                        step(v.tensor_scalar(tried, steps_iota[:, first, :], base, None, ALU.add))
                        step(v.tensor_tensor(compare_buf, key.rearrange("p (o t) -> p o t", o=1).broadcast_to((P, FAN, TILES)),
                                             tried.rearrange("p (j o) -> p j o", o=1).broadcast_to((P, FAN, TILES)), ALU.is_ge))
                        v.tensor_reduce(search[:, 16:16 + FAN], compare_buf, AX.X, ALU.add).then_inc(totals_in, 1)
                        total_of(FAN)
                        step(v.tensor_scalar(search[:, 48:48 + FAN], psum[:, 7, 0:FAN], need, 0.0, ALU.is_ge, ALU.add, accum_out=count))
                        step(v.tensor_scalar(count, count, -1.0, float(size), ALU.add, ALU.mult))
                        step(v.tensor_tensor(base, base, count, ALU.add))
                    v.tensor_scalar(above, key, base, 0.0, ALU.is_gt, ALU.add, accum_out=search[:, 16:17]).then_inc(totals_in, 1)
                    total_of(1)
                    step(v.tensor_tensor(need, need, psum[:, 7, 0:1], ALU.subtract))
                    step(v.tensor_tensor(chosen, chosen, above, ALU.add))
                    step(v.tensor_scalar(equal, key, base, None, ALU.is_equal))
                step(v.tensor_tensor(chosen, chosen, equal, ALU.add))
                v.tensor_copy(kept16[:], chosen).then_inc(kept_ready, 1)
                dve.wait_ge(kept_ready, level + 2)

            spread = [0, 0]
            for i, (kind, level, slot, slots, norm) in enumerate(CONVS):
                unit, v = FIRST_UNIT + i, nc.vector
                if i in POOLED:
                    choose(level - 1)
                    degrees(level)
                if i in UNSCALED:
                    step(v.tensor_reduce(bounds[:, slot:slot + 1], nodes_t, AX.X, ALU.max, apply_absolute_value=True))
                    v.tensor_scalar(abs_w.bitcast(I32), weights[:].bitcast(I32), 0x7FFFFFFF, None, ALU.bitwise_and).then_inc(abs_ready, 1)
                    dve.wait_ge(bound_ready, 2 + UNSCALED.index(i))
                    fit_powers(i, i + 1, psum[:, 7, 16 + i:17 + i])
                    fit_weights(i)
                for t in range(TILES):
                    dve.wait_ge(hi_ready, TILES * i + min(t - t % 4 + 4, TILES))
                    v.scalar_tensor_tensor(parts0[:, t, 1, :], psum[:, 4 + t // 4 % 4, (t % 4) * P:(t % 4 + 1) * P],
                                           dcol[:, level, 0, t:t + 1], parts0[:, t, 0, :], ALU.mult, ALU.subtract
                                           ).then_inc(lo_ready, 1)
                if i == 0 or CONVS[i - 1][1] != level:
                    spread[0] += 1
                    dve.wait_ge(db_in, DMA * spread[0])
                    if level > 0:
                        spread[1] += 1
                        dve.wait_ge(kb_in, DMA * spread[1])
                blocks_of(unit, 0, BLOCKS, lambda b: v.scalar_tensor_tensor(
                    agg_t[:, b * BLOCK:(b + 1) * BLOCK], psum[:, b, 0:BLOCK], unfit[:, i:i + 1], d_all[:, b * BLOCK:(b + 1) * BLOCK],
                    ALU.mult, ALU.mult))
                dve.wait_ge(blocks_out, BLOCKS * (unit + 1))
                real = agg_t[:, 0:NODES] if level == 0 else agg_t[:, 0:COLS]
                kept = k_all
                if norm is None:
                    bias = vec({"in": V_IN_B, "bot": V_BOT_B, "out": V_OUT_B}[kind])
                    if kind == "in":
                        step(v.tensor_scalar(nodes_t[:, 0:COLS], agg_t[:, 0:COLS], bias, None, ALU.add))
                    elif kind == "bot":
                        step(v.tensor_scalar(agg_t[:, 0:COLS], agg_t[:, 0:COLS], bias, 0.0, ALU.add, ALU.max))
                        dve.wait_ge(xs_out, DMA * 3)
                        step(v.tensor_tensor(nodes_t[:, 0:COLS], agg_t[:, 0:COLS], kept, ALU.mult))
                    else:
                        step(v.tensor_scalar(agg_t[:, 0:COLS], agg_t[:, 0:COLS], bias, None, ALU.add))
                else:
                    g, beta, bias = ((V_DN_G, V_DN_BETA, V_DN_B) if kind == "dn" else (V_UP_G, V_UP_BETA, V_UP_B))
                    total, minus_mean, inv, gain, half, sq = (bn[:, k:k + 1] for k in range(6))
                    if level == 0:
                        step(v.tensor_scalar(real, real, vec(bias + norm), 0.0, ALU.add, ALU.add, accum_out=total))
                    else:
                        step(v.scalar_tensor_tensor(real, real, vec(bias + norm), kept, ALU.add, ALU.mult, accum_out=total))
                    step(v.tensor_scalar(minus_mean, total, -1.0 / LEVEL_NODES[level], None, ALU.mult))
                    if level == 0:
                        v.tensor_scalar(real, real, minus_mean, None, ALU.add).then_inc(v_centered, 1)
                    else:
                        v.scalar_tensor_tensor(real, real, minus_mean, kept, ALU.add, ALU.mult).then_inc(v_centered, 1)
                    normed = sum(c[4] is not None for c in CONVS[:i]) + 1
                    dve.wait_ge(v_squared, normed)
                    step(v.tensor_scalar(inv, sq, 1.0 / LEVEL_NODES[level], 1e-5, ALU.mult, ALU.add))
                    rsqrt(gain, inv, half)
                    v.tensor_tensor(gain, gain, vec(g + norm), ALU.mult).then_inc(coef_ready, 1)
                    dve.wait_ge(relu_done, normed)
                    if level > 0:
                        step(v.tensor_tensor(nodes_t[:, 0:COLS], nodes_t[:, 0:COLS], kept, ALU.mult))
                if kind != "out":
                    v.memset(nodes_t[:, COLS:PAD], 0.0).then_inc(xt_ready, 1)
                    dve.wait_ge(xt_ready, i + 1)
                else:
                    v.memset(agg_t[:, COLS:PAD], 0.0).then_inc(xt_ready, 1)
            for g, (t0, n) in enumerate(GROUPS4):
                dve.wait_ge(final_turned, g + 1)
                nc.vector.tensor_tensor(nodebuf[:, t0 * P:(t0 + n) * P], nodebuf[:, t0 * P:(t0 + n) * P],
                                        psum[:, g, 0:n * P], ALU.add).then_inc(final_ready, 1)

        @block.scalar
        def _(act):
            act.dma_start(vec_rows[V_IN_B:V_IN_B + 1, :], row_of(a["L1_gnn_in_b"])).then_inc(weights_in, DMA)
            for row, name in ((V_DN_B, "dn_b"), (V_DN_G, "dn_g"), (V_DN_BETA, "dn_beta"), (V_POOL, "pool_w"),
                              (V_UP_B, "up_b"), (V_UP_G, "up_g"), (V_UP_BETA, "up_beta")):
                act.dma_start(vec_rows[row:row + 3, :], a["L1_gnn_" + name]).then_inc(weights_in, DMA)
            act.dma_start(vec_rows[V_BOT_B:V_BOT_B + 1, :], row_of(a["L1_gnn_bot_b"])).then_inc(weights_in, DMA)
            act.dma_start(vec_rows[V_OUT_B:V_OUT_B + 1, :], row_of(a["L1_gnn_out_b"])).then_inc(weights_in, DMA)
            act.dma_start(weights[:, 0, :], a["L1_gnn_in_W"]).then_inc(weights_in, DMA)
            act.dma_start(weights[:, 1:4, :], a["L1_gnn_dn_W"].rearrange("s k f -> k s f")).then_inc(weights_in, DMA)
            act.dma_start(weights[:, 4, :], a["L1_gnn_bot_W"]).then_inc(weights_in, DMA)
            act.dma_start(weights[:, 5:11, :], a["L1_gnn_up_W"].rearrange("s (h k) f -> k (s h) f", h=2)).then_inc(weights_in, DMA)
            act.dma_start(weights[:, 11, :], a["L1_gnn_out_W"]).then_inc(weights_in, DMA)
            act.wait_ge(pads_zeroed, 1)
            load_x(act, x_in)
            act.wait_ge(centered, 1)
            nc.scalar.activation(region3[:, 0:PAD], nodebuf[:], ACT.Square).then_inc(squared, 1)
            act.wait_ge(h0_ready, 1)
            nc.scalar.activation(region3[:, 0:PAD], nodebuf[:], ACT.Square).then_inc(h0_squared, 1)
            act.wait_ge(scaled0, 1)
            nc.scalar.activation(parts0[:, :, 0, :], tiles(region3[:, PAD:2 * PAD]), ACT.Copy).then_inc(hi0_ready, 1)
            act.wait_ge(parts0_ready, 1)
            act.dma_start(wl0[:], a["L0_gnn_Wl0"]).then_inc(w2_ready, DMA)
            act.dma_start(wr0[:], a["L0_gnn_Wr0"]).then_inc(w2_ready, DMA)
            act.dma_start(wl1[:], a["L0_gnn_Wl1"].rearrange("(m k) f -> k m f", m=2)).then_inc(w2_ready, DMA)
            act.dma_start(wr1[:], a["L0_gnn_Wr1"].rearrange("(m k) f -> k m f", m=2)).then_inc(w2_ready, DMA)
            act.dma_start(bias0[:], row_of(a["L0_gnn_bl0"]).broadcast_to((P, 256))).then_inc(w2_ready, DMA)
            act.dma_start(bias1[:], row_of(a["L0_gnn_bl1"]).broadcast_to((P, P))).then_inc(w2_ready, DMA)
            act.dma_start(scales[:, 0:1], row_of(a["L0_gnn_scale0"]).broadcast_to((P, 1))).then_inc(w2_ready, DMA)
            act.dma_start(scales[:, 1:2], row_of(a["L0_gnn_scale1"]).broadcast_to((P, 1))).then_inc(w2_ready, DMA)
            for g in range(GROUPS):
                for k in range(2):
                    act.wait_ge(turned, 2 * g + k + 1)
                    nc.scalar.activation(by_edge[:, k, :, g * P:(g + 1) * P],
                                         psum[:, 2 * (g % 2) + k, 0:CHUNKS * P].rearrange("p (c w) -> p c w", c=CHUNKS),
                                         ACT.Copy).then_inc(by_edge_ready, 1)
            for g, (t0, n) in enumerate(GROUPS4):
                act.wait_ge(h0_turned, g + 1)
                nc.scalar.activation(h0t[:, t0 * P:(t0 + n) * P], psum[:, g % 4, 0:n * P], ACT.Copy).then_inc(h0t_ready, 1)
            act.sem_inc(bank_free, 4)
            act.wait_ge(consts_ready, 5)
            with act.Fori(0, ITS) as it:
                for b in range(4):
                    act.wait_ge(window_done, 8 * it + (RING + 2 * b + 2))
                    act.wait_ge(stage_free, 4 * it + (b + 1))
                    act.wait_ge(bank_free, 4 * it + (b + 1))
                    nc.scalar.activation(relu_out[:, b], psum[:, 4 + b, 0:2 * KEYS], ACT.Relu, bias=minus15[:],
                                         accum_out=excess[:, bass.ds(4 * it + b, 1)])
                    nc.scalar.activation(stage[:, b].rearrange("p t (w j) -> p w t j", w=2),
                                         psum[:, 4 + b, 0:2 * KEYS].rearrange("p (w t j) -> p w t j", w=2, t=TILES),
                                         ACT.Copy, saturate=False).then_inc(bank_free, 1)

            act.wait_ge(blocks_out, BLOCKS)
            act.wait_ge(agg_zeroed, 1)
            nc.scalar.activation(squares, agg0t, ACT.Square).then_inc(sq_ready, 1)
            for t in range(TILES):
                act.wait_ge(proj_done, t + 1)
                last = nc.scalar.activation(junk0[:, t, :], out0[:, t, :], ACT.Square, accum_out=tiny[:, 8, t:t + 1])
            last.then_inc(ss_ready, 1)
            act.wait_ge(h1_ready, 1)
            for t in range(TILES):
                last = nc.scalar.activation(junk1[:, t, :], out0[:, t, :], ACT.Square, accum_out=tiny[:, 8, t:t + 1])
            last.then_inc(h1_squared, 1)
            act.wait_ge(rns_ready, 1)
            for t in range(TILES):
                nc.scalar.activation(parts1[:, t, 0, :], out0[:, t, :], ACT.Copy, scale=tiny[:, 4, t:t + 1]).then_inc(hi1_ready, 1)
                if t % 2 or t == TILES - 1:
                    g = t // 2
                    t0, n = GROUPS2[g]
                    act.wait_ge(h1_turned, g + 1)
                    nc.scalar.activation(h1t[:, :, t0 * P:(t0 + n) * P],
                                         psum[:, g % 4, 0:2 * n * P].rearrange("p (m n) -> p m n", m=2), ACT.Copy).then_inc(h1t_ready, 1)
            act.wait_ge(blocks_out, 3 * BLOCKS)
            act.wait_ge(agg_zeroed, 3)
            nc.scalar.activation(squares1, agg1t, ACT.Square).then_inc(sq_ready, 1)
            act.wait_ge(norm_ready, 2)
            for t in range(TILES):
                act.wait_ge(proj_done, TILES + t + 1)
                last = nc.scalar.activation(junk2[:, t, :], tiles(out1)[:, t, :], ACT.Square, accum_out=tiny[:, 8, t:t + 1])
            last.then_inc(ss_ready, 1)
            act.wait_ge(centered, 2)
            nc.scalar.activation(region1[:, 0:PAD], out1, ACT.Square).then_inc(squared, 1)
            for g, (t0, n) in enumerate(GROUPS4):
                act.wait_ge(h2_turned, g + 1)
                nc.scalar.activation(nodes_t[:, t0 * P:(t0 + n) * P], psum[:, g % 4, 0:n * P], ACT.Copy).then_inc(h2t_ready, 1)
            normed = 0
            for i, (kind, level, slot, slots, norm) in enumerate(CONVS):
                for t in range(TILES):
                    act.wait_ge(hw_ready, len(GROUPS4) * i + t // 4 + 1)
                    nc.scalar.activation(parts0[:, t, 0, :], psum[:, 4 + t // 4 % 4, (t % 4) * P:(t % 4 + 1) * P], ACT.Copy,
                                         scale=dcol[:, level, 0, t:t + 1]).then_inc(hi_ready, 1)
                if norm is not None:
                    normed += 1
                    real = NODES if level == 0 else COLS
                    act.wait_ge(v_centered, normed)
                    nc.scalar.activation(squares[:, 0:real], agg_t[:, 0:real], ACT.Square, accum_out=bn[:, 5:6]).then_inc(v_squared, 1)
                    act.wait_ge(coef_ready, normed)
                    if kind == "dn" and level > 0:
                        act.wait_ge(xs_out, DMA * level)
                    beta = (V_DN_BETA if kind == "dn" else V_UP_BETA) + norm
                    nc.scalar.activation(nodes_t[:, 0:real], agg_t[:, 0:real], ACT.Relu, bias=vecs[:, beta:beta + 1],
                                         scale=bn[:, 3:4]).then_inc(relu_done, 1)

        def input_bound(pe, i):
            _, _, slot, slots, _ = CONVS[i]
            for k in range(slots):
                last = pe.matmul(psum[:, 7, 16 + i:17 + i], abs_w[:, slot + k, :], bounds[:, slot + k:slot + k + 1],
                                 start=(k == 0), stop=(k == slots - 1))
            return last

        def fit_row(pe, n):
            pe.wait_ge(diag_ready, n + 1)
            pe.matmul(psum[:, 7, 0:P], ones[:], diag_fit, start=True, stop=True).then_inc(row_ready, 1)

        @block.tensor
        def _(pe):
            pe.wait_ge(consts_ready, 11)
            pe.wait_ge(weights_in, N_WEIGHTS * DMA)
            pe.transpose(psum[:, 7, 0:V_ROWS], vec_rows[:], ident[0:V_ROWS, 0:V_ROWS]).then_inc(vec_turned, 1)
            pe.wait_ge(abs_ready, 1)
            pe.matmul(psum[:, 7, 32:35], ones[:], search[:, 0:3], start=True, stop=True)
            for i in range(len(CONVS)):
                bound = input_bound(pe, i)
            bound.then_inc(bound_ready, 1)
            for n, i in enumerate(i for i in range(len(CONVS)) if i not in UNSCALED):
                fit_row(pe, n)
            for g in range(GROUPS):
                pe.wait_ge(keyed, g + 1)
                for k, rows in enumerate((lo_rows, key_rows)):
                    if g >= 2:
                        pe.wait_ge(by_edge_ready, 2 * (g - 2) + k + 1)
                    for c in range(CHUNKS):
                        last = pe.transpose(psum[:, 2 * (g % 2) + k, c * P:(c + 1) * P], rows[:, g, c * P:(c + 1) * P], ident[:])
                    last.then_inc(turned, 1)
            for g, (t0, n) in enumerate(GROUPS4):
                pe.wait_ge(by_edge_ready, 2 * GROUPS)
                if g >= 4:
                    pe.wait_ge(h0t_ready, g - 3)
                for t in range(t0, t0 + n):
                    last = pe.transpose(psum[:, g % 4, (t - t0) * P:(t - t0 + 1) * P], nodebuf[:, t * P:(t + 1) * P], ident[:])
                last.then_inc(h0_turned, 1)
            pe.sem_inc(window_done, RING)
            with pe.Fori(0, ITS) as it:
                for w in range(PER_IT):
                    pe.wait_ge(hot_ready, 8 * it + (w + 2))
                    if w % 2 == 0:
                        pe.wait_ge(bank_free, 4 * it + (w // 2 + 1))
                    for c in range(CHUNKS):
                        last = pe.matmul(psum[:, 4 + w // 2, (w % 2) * KEYS:(w % 2 + 1) * KEYS], hot_lo[:, w % RING, c, :],
                                         hot_key[:, w % RING, c, :], start=(c == 0), stop=(c == CHUNKS - 1))
                    last.then_inc(window_done, 1)


            def aggregate(unit, weight, ready, first):
                for half, (b0, b1) in enumerate(((0, 4), (4, BLOCKS))):
                    if unit > 0:
                        pe.wait_ge(blocks_out, BLOCKS * (unit - 1) + (4 if half == 0 else BLOCKS))
                    for t in range(TILES):
                        if half == 0 and ready is not None:
                            pe.wait_ge(ready, first + t)
                        for k in range(2):
                            for b in range(b0, b1):
                                last = pe.matmul(psum[:, b, 0:BLOCK], weight(t, k),
                                                 adj[:, t * PAD + b * BLOCK:t * PAD + (b + 1) * BLOCK],
                                                 start=(t == 0 and k == 0), stop=(t == TILES - 1 and k == 1))
                    last.then_inc(agg_half, 1)

            def row_norms(pairs):
                for t in range(TILES):
                    for m, sq in enumerate(pairs):
                        last = pe.matmul(psum[:, 7, t:t + 1], sq[:, t * P:(t + 1) * P], ones[:, 0:1],
                                         start=(m == 0), stop=(m == len(pairs) - 1))
                last.then_inc(norm_ready, 1)

            def project(layer, sums, rows, wl, wr, width):
                for t in range(TILES):
                    m = layer * TILES + t
                    if t >= 4:
                        pe.wait_ge(proj_done, m - 3)
                    for col, lhs, w in ((0, sums, wl), (256, rows, wr)):
                        for k in range(len(lhs)):
                            last = pe.matmul(psum[:, t % 4, col:col + width], lhs[k][:, t * P:(t + 1) * P], w[k],
                                             start=(k == 0), stop=(k == len(lhs) - 1))
                    last.then_inc(proj_ready, 1)

            def degree_sums(level):
                pe.wait_ge(kept_ready, level + 1)
                for d in range(TILES):
                    for t in range(TILES):
                        last = pe.matmul(psum[:, 7, d:d + 1], adj[:, t * PAD + d * P:t * PAD + (d + 1) * P], kept16[:, t:t + 1],
                                         start=(t == 0), stop=(t == TILES - 1))
                last.then_inc(deg_ready, 1)

            def turn_degrees(level):
                pe.wait_ge(dk_ready, level + 1)
                pe.transpose(psum[0:2 * TILES, 7, P:2 * P], dcol[:, level].rearrange("p v t -> p (v t)"), ident[:]).then_inc(dk_turned, 1)

            pe.wait_ge(adj_ready, 2)
            pe.wait_ge(parts0_ready, 1)
            aggregate(0, lambda t, k: parts0[:, t, k, :], None, 0)
            pe.wait_ge(sq_ready, 1)
            row_norms([squares])
            pe.wait_ge(blocks_out, BLOCKS)
            pe.wait_ge(w2_ready, 8 * DMA)
            project(0, [agg0t], [h0t], [wl0[:]], [wr0[:]], 256)
            pe.wait_ge(h1_ready, 1)
            for g, (t0, n) in enumerate(GROUPS2):
                if g >= 4:
                    pe.wait_ge(h1t_ready, g - 3)
                for m in range(2):
                    for t in range(t0, t0 + n):
                        last = pe.transpose(psum[:, g % 4, (m * n + t - t0) * P:(m * n + t - t0 + 1) * P],
                                            out0[:, t, m * P:(m + 1) * P], ident[:])
                last.then_inc(h1_turned, 1)
            pe.wait_ge(h1t_ready, len(GROUPS2))
            for m in range(2):
                aggregate(1 + m, lambda t, k: parts1[:, t, k, m * P:(m + 1) * P], lo1_ready if m == 0 else None, 1)
            pe.wait_ge(sq_ready, 2)
            row_norms([squares1[:, 0, :], squares1[:, 1, :]])
            project(1, [agg1t[:, 0, :], agg1t[:, 1, :]], [h1t[:, 0, :], h1t[:, 1, :]],
                    [wl1[:, 0, :], wl1[:, 1, :]], [wr1[:, 0, :], wr1[:, 1, :]], P)
            degree_sums(0)
            pe.wait_ge(h2_ready, 1)
            for g, (t0, n) in enumerate(GROUPS4):
                if g >= 4:
                    pe.wait_ge(h2t_ready, g - 3)
                for t in range(t0, t0 + n):
                    last = pe.transpose(psum[:, g % 4, (t - t0) * P:(t - t0 + 1) * P], out1[:, t * P:(t + 1) * P], ident[:])
                last.then_inc(h2_turned, 1)
            turn_degrees(0)

            totals = 0
            up = 0
            for i, (kind, level, slot, slots, norm) in enumerate(CONVS):
                if i == 0:
                    pe.wait_ge(h2t_ready, len(GROUPS4))
                else:
                    pe.wait_ge(xt_ready, i)
                if i in POOLED:
                    for t in range(TILES):
                        last = pe.matmul(psum[:, 7, t:t + 1], nodes_t[:, t * P:(t + 1) * P], vecs[:, V_POOL + level - 1:V_POOL + level],
                                         start=True, stop=True)
                    last.then_inc(score_ready, 1)
                    for _, steps in key_steps(level - 1):
                        for n in [FAN] * len(steps) + [1]:
                            totals += 1
                            pe.wait_ge(totals_in, totals)
                            pe.matmul(psum[:, 7, 0:n], ones[:], search[:, 16:16 + n], start=True, stop=True).then_inc(totals_out, 1)
                    degree_sums(level)
                    turn_degrees(level)
                if i in UNSCALED:
                    n = UNSCALED.index(i)
                    pe.wait_ge(abs_ready, 2 + n)
                    input_bound(pe, i).then_inc(bound_ready, 1)
                    fit_row(pe, len(CONVS) - len(UNSCALED) + n)
                pe.wait_ge(dkrows_ready, max(c[1] for c in CONVS[:i + 1]) + 1)
                if kind == "up":
                    up += 1
                    pe.wait_ge(xs_in, DMA * up)
                pe.wait_ge(weights_fit, len(CONVS) - len(UNSCALED) + sum(u <= i for u in UNSCALED))
                inputs = [nodes_t, skip_t][:slots]
                for g, (t0, n) in enumerate(GROUPS4):
                    if g >= 4:
                        pe.wait_ge(lo_ready, TILES * i + 4 * (g - 3))
                    for t in range(t0, t0 + n):
                        for k, x in enumerate(inputs):
                            last = pe.matmul(psum[:, 4 + g % 4, (t - t0) * P:(t - t0 + 1) * P], x[:, t * P:(t + 1) * P],
                                             weights[:, slot + k, :], start=(k == 0), stop=(k == slots - 1))
                    last.then_inc(hw_ready, 1)
                aggregate(FIRST_UNIT + i, lambda t, k: parts0[:, t, k, :], lo_ready, TILES * i + 1)
            pe.wait_ge(xt_ready, len(CONVS))
            for g, (t0, n) in enumerate(GROUPS4):
                for t in range(t0, t0 + n):
                    last = pe.transpose(psum[:, g, (t - t0) * P:(t - t0 + 1) * P], agg_t[:, t * P:(t + 1) * P], ident[:])
                last.then_inc(final_turned, 1)


_INS = ["x", "src", "dst", "L0_gnn_Wl0", "L0_gnn_bl0", "L0_gnn_Wr0", "L0_gnn_Wl1", "L0_gnn_bl1", "L0_gnn_Wr1",
        "L0_gnn_scale0", "L0_gnn_scale1", "L1_gnn_in_W", "L1_gnn_in_b", "L1_gnn_dn_W", "L1_gnn_dn_b", "L1_gnn_dn_g",
        "L1_gnn_dn_beta", "L1_gnn_pool_w", "L1_gnn_bot_W", "L1_gnn_bot_b", "L1_gnn_up_W", "L1_gnn_up_b", "L1_gnn_up_g",
        "L1_gnn_up_beta", "L1_gnn_out_W", "L1_gnn_out_b"]


def kernel(**inputs):
    import numpy as np
    import concourse.bacc as bacc
    from concourse.bass_utils import run_bass_kernel_spmd

    nc = bacc.Bacc("TRN2", target_bir_lowering=False, num_devices=1)
    arrays, args = {}, {}
    for name in _INS:
        x = np.ascontiguousarray(inputs[name]).reshape(inputs[name].shape or (1,))
        arrays["in_" + name] = x
        args[name] = nc.dram_tensor("in_" + name, x.shape, mybir.dt.from_np(x.dtype), kind="ExternalInput").ap()
    out = nc.dram_tensor("out", (NODES, FEAT), F32, kind="ExternalOutput").ap()
    gnn_kernel(nc, args, out)
    return run_bass_kernel_spmd(nc, [arrays], core_ids=[0]).results[0]["out"]
```

```python
from contextlib import ExitStack

import concourse.bass as bass
from concourse import mybir

ALU = mybir.AluOpType
ACT = mybir.ActivationFunctionType
AX = mybir.AxisListType
F32 = mybir.dt.float32
F16 = mybir.dt.float16
BF16 = mybir.dt.bfloat16
FP8 = mybir.dt.float8e4
I32 = mybir.dt.int32
U32 = mybir.dt.uint32

P = 128
NODES, FEAT, EDGES = 3125, 128, 100000
TILES = -(-NODES // P)
TAIL = NODES - (TILES - 1) * P
PAD = TILES * P

BLOCKS = 7
BLOCK = 448
COLS = BLOCKS * BLOCK
assert NODES <= COLS <= PAD

WIN = 8
WINDOWS = COLS // WIN
SLOTS = 384
CHUNKS = SLOTS // P
GRAIN = 32
ROWS = (EDGES - SLOTS) // GRAIN + 1
GROUPS = 4
KEYS = TILES * WIN
CHUNK_DESTS = ((0, 6), (0, WIN), (5, WIN))
LATE_WINDOWS = (NODES - 1) // WIN
PER_IT = 28
ITS = WINDOWS // PER_IT
PAIRS = PER_IT // 2
STAGE = 7
COUNT = 0.125
FULL = 0x40404040
RING = 14
EP, EC = 125, 800
DMA = 16
GEN_STEPS = EC + TILES
SUMS = [("agg", 0), ("agg", 1), ("agg", 2), ("deg", 0), ("agg", 3), ("agg", 4), ("deg", 1), ("agg", 5), ("deg", 2),
        ("agg", 6), ("deg", 3)] + [("agg", u) for u in range(7, 12)]

LEVEL_NODES = (NODES, NODES // 2, NODES // 4, NODES // 8)
CONVS = (("in", 0, 0, 1, None), ("dn", 0, 1, 1, 0), ("dn", 1, 2, 1, 1), ("dn", 2, 3, 1, 2), ("bot", 3, 4, 1, None),
         ("up", 2, 5, 2, 0), ("up", 1, 7, 2, 1), ("up", 0, 9, 2, 2), ("out", 0, 11, 1, None))
W_SLOTS = 12
POOLED = (2, 3, 4)
UNSCALED = (1, 5)
FIRST_UNIT = 3
V_IN_B, V_DN_B, V_DN_G, V_DN_BETA, V_POOL, V_BOT_B, V_UP_B, V_UP_G, V_UP_BETA, V_OUT_B = 0, 1, 4, 7, 10, 13, 14, 17, 20, 23
V_ROWS = 24
HALF = 12 * P
UNIT_SCALE = 8192.0
RSQRT_MAGIC = 1597463007.0
GROUPS4 = [(t, min(4, TILES - t)) for t in range(0, TILES, 4)]
GROUPS2 = [(t, min(2, TILES - t)) for t in range(0, TILES, 2)]
TANH_CLAMP = 7.99881172180175781
BELOW_1 = 1.0 - 2.0 ** -24
TANH_P = (-2.76076847742355e-16, 2.00018790482477e-13, -8.60467152213735e-11, 5.12229709037114e-08,
          1.48572235717979e-05, 6.37261928875436e-04, 4.89352455891786e-03)
TANH_Q = (1.19825839466702e-06, 1.18534705686654e-04, 2.26843463243900e-03, 4.89352518554385e-03)
FAN = 16

WHOLE_STEPS = (4096, 256, 16, 1)
INDEX_STEPS = WHOLE_STEPS[1:]


def score_keys(level):
    return [(2 * level + half, WHOLE_STEPS) for half in range(2)]


def tie_keys(level):
    return [k for lv in range(level - 1, -1, -1) for k in score_keys(lv)] + [(6, INDEX_STEPS)]


def gnn_kernel(nc, a, out):
    with ExitStack() as ctx:
        def sb(name, shape, dt):
            return ctx.enter_context(nc.sbuf_tensor(name, shape, dt))

        def sem(name):
            return ctx.enter_context(nc.semaphore(name))

        def dram(name, shape, dt):
            return nc.dram_tensor(name, shape, dt, kind="Internal").ap()

        last_row = dram("last_row", (EDGES // GRAIN,), F32)
        src_table = dram("src_table", (ROWS, SLOTS), I32)
        dst_table = dram("dst_table", (ROWS, SLOTS), I32)

        dk_dram = dram("dk_dram", (4, 2 * TILES, P), F32)
        xs_dram = dram("xs_dram", (3, P, PAD), F32)

        gen_table = {n: dram(f"gen_table{n}", (PAD, n), F16) for n in (256, 512)}

        adj = sb("adj", [P, TILES * PAD], FP8)
        region1 = sb("region1", [P, 6400], F32)
        region2 = sb("region2", [P, 6400], F32)
        region3 = sb("region3", [P, 6400], F32)
        ident = sb("ident", [P, P], F32)
        iota_lo = sb("iota_lo", [P, P], BF16)
        iota_key = sb("iota_key", [P, KEYS], BF16)
        win_base = sb("win_base", [P, GROUPS], F32)
        scalars = sb("scalars", [P, 2, PER_IT, CHUNKS], F32)
        row_f = sb("row_f", [P, GROUPS], F32)
        row_i = sb("row_i", [P, GROUPS], U32)
        uncovered = sb("uncovered", [P, 2 * GROUPS], F32)
        chunk2_dest = sb("chunk2_dest", [P, GROUPS], F32)

        parts = sb("parts", [P, 6400], F32)
        nodebuf = sb("nodebuf", [P, PAD], F32)
        weights = sb("weights", [P, W_SLOTS, P], F32)
        scales = sb("scales", [P, 2], F32)
        vec_rows = sb("vec_rows", [V_ROWS, P], F32)
        vecs = sb("vecs", [P, V_ROWS], F32)
        ones = sb("ones", [P, P], F32)
        bounds = sb("bounds", [P, W_SLOTS], F32)
        fit = sb("fit", [P, 9], F32)
        unfit = sb("unfit", [P, 9], F32)
        bn = sb("bn", [P, 10], F32)
        block_sums = sb("block_sums", [P, BLOCKS], F32)
        tiny = sb("tiny", [P, 12, TILES], F32)
        dcol = sb("dcol", [P, 4, 2, TILES], F32)
        kept16 = sb("kept16", [P, TILES], BF16)
        keys = sb("keys", [P, 7, TILES], F32)
        pool_norm = sb("pool_norm", [P, 3], F32)
        steps_iota = sb("steps_iota", [P, 4, FAN], F32)
        search = sb("search", [P, 64], F32)
        compare_buf = parts[:, 3200:3200 + FAN * TILES].rearrange("p (j t) -> p j t", j=FAN)
        key_work = parts[:, 3700:3700 + 8 * TILES].rearrange("p (k t) -> p k t", k=8)
        dk_rows = parts[0:2 * TILES, 4000:4000 + P]

        flag = sb("flag", [P, 1], I32)
        tie = sb("tie", [P, 1], I32)
        spare = sb("spare", [P, 1], F32)
        words = adj[:, :].bitcast(F32)
        gen_cols = words[:, 0:COLS]
        gen_hot = words[:, 3200:3200 + COLS // 2].bitcast(BF16)
        gen_rows = words[:, 4800:5056].bitcast(F16)
        gen_kept = words[:, 5100:8300].bitcast(F16).rearrange("p (t c) -> p t c", t=TILES)
        gen_degrees = words[:, 8300:8300 + PAD]
        gen_src = words[:, 11500:11501].bitcast(I32)
        gen_spare = words[:, 11504:11505]
        gen_all_src, gen_all_dst = (words[:, 12000 + EC * k:12000 + EC * (k + 1)].bitcast(I32) for k in range(2))
        gen_dst_f = words[:, 11502:11503]
        gen_nodes = words[:, 11510:11510 + TILES]

        def halves(level):
            return (0, HALF), (HALF, NODES if level == 0 else COLS)

        def tiles(ap):
            return ap.rearrange("p (t f) -> p t f", t=TILES)

        def per_node(col, n=FEAT):
            return col.rearrange("p (t o) -> p t o", o=1).broadcast_to((P, TILES, n))

        wl0, wr0, bias0 = (region3[:, 3600 + 256 * k:3856 + 256 * k] for k in range(3))
        wl1, wr1 = (region3[:, 4368 + 256 * k:4624 + 256 * k].rearrange("p (m f) -> p m f", m=2) for k in range(2))
        bias1 = region3[:, 4880:5008]
        h0t, agg0t = region2[:, 0:PAD], region2[:, PAD:2 * PAD]
        parts0 = parts[:, 0:3200].bitcast(F16).rearrange("p (t k f) -> p t k f", t=TILES, k=2)
        parts1 = parts[:, :].bitcast(F16).rearrange("p (t k f) -> p t k f", t=TILES, k=2)
        squares = parts[:, 3200:6400]
        out0 = region1[:, :].rearrange("p (t f) -> p t f", t=TILES)
        h1t = region2[:, :].rearrange("p (m n) -> p m n", m=2)
        agg1t = region1[:, :].rearrange("p (m n) -> p m n", m=2)
        squares1 = parts[:, :].rearrange("p (m n) -> p m n", m=2)
        junk0 = parts[:, 3200:6400].bitcast(BF16).rearrange("p (t f) -> p t f", t=TILES)
        junk1 = region3[:, 0:3200].bitcast(BF16).rearrange("p (t f) -> p t f", t=TILES)
        junk2 = parts[:, 0:1600].bitcast(BF16).rearrange("p (t f) -> p t f", t=TILES)
        proj_tmp = region3[:, 6400 - 512:6400].rearrange("p (r f) -> p r f", r=2)
        out1 = region3[:, 0:PAD]
        nodes_t = region2[:, 0:PAD]
        agg_t = region2[:, PAD:2 * PAD]
        skip_t = region1[:, 0:PAD]
        d_all = region1[:, PAD:PAD + COLS]
        k_all = region3[:, 0:COLS]
        abs_w = parts[:, 3200:3200 + W_SLOTS * P].rearrange("p (s f) -> p s f", s=W_SLOTS)
        diag_fits = region1[:, 4800:4800 + 7 * P].rearrange("p (n f) -> p n f", n=7)
        diag_fit = parts[:, 4800:4800 + P]

        dst_in = region1[0:EP, 0:EC].bitcast(I32)
        last_in = region1[0:EP, EC:EC + EC // GRAIN]
        last_all = region1[:, 1024:1024 + EDGES // GRAIN]
        compared = region2[:, 0:EDGES // GRAIN]
        edge_src = region2[:, 3200:3200 + GROUPS * SLOTS].bitcast(I32).rearrange("p (g s) -> p g s", g=GROUPS)
        edge_dst = region2[:, 4800:4800 + GROUPS * SLOTS].bitcast(I32).rearrange("p (g s) -> p g s", g=GROUPS)
        work = [region1[:, 4352 + SLOTS * k:4352 + SLOTS * (k + 1)] for k in range(4)]
        lo_rows = region2[:, 0:GROUPS * SLOTS].rearrange("p (g s) -> p g s", g=GROUPS)
        key_rows = region2[:, 1600:1600 + GROUPS * SLOTS].rearrange("p (g s) -> p g s", g=GROUPS)
        by_edge = region1[:, 0:2 * CHUNKS * 512].rearrange("p (k w c) -> p k w c", k=2, c=CHUNKS)
        hot_lo = region3[:, 0:RING * CHUNKS * 64].bitcast(BF16).rearrange("p (r c n) -> p r c n", r=RING, c=CHUNKS)
        hot_key = region1[:, 3072:3072 + RING * 200].bitcast(BF16).rearrange("p (r c n) -> p r c n", r=RING, c=2)
        hot_key2 = parts[:, 3200:3200 + RING * 100].bitcast(BF16).rearrange("p (r n) -> p r n", r=RING)
        stage = region2[:, 3200:3200 + 1400].bitcast(FP8).rearrange("p (s t n) -> p s t n", s=2, t=TILES)
        stage_words = region2[:, 3200:3200 + 1400].bitcast(U32).rearrange("p (s t n) -> p s t n", s=2, t=TILES)
        seen = region2[:, 4800:4800 + TILES * PER_IT].bitcast(U32).rearrange("p (t n) -> p t n", t=TILES)
        loops = region2[:, 5600:5600 + P]
        lo_distance = region1[:, 5900:5900 + P].bitcast(BF16).rearrange("p (w n) -> p w n", w=2)
        first_los = region1[:, 6100:6100 + PER_IT].rearrange("p (w o) -> p w o", o=1)
        adj_words = adj[:, :].bitcast(U32).rearrange("p (t n) -> p t n", t=TILES)

        psum = ctx.enter_context(nc.psum_tensor("psum", [P, 8, 512], F32))

        edges_in = sem("edges_in")
        table_in = sem("table_in")
        last_picked = sem("last_picked")
        last_out = sem("last_out")
        last_back = sem("last_back")
        pool_step = sem("pool_step")
        consts_ready = sem("consts_ready")
        rows_known = sem("rows_known")
        gathered = [sem(f"gathered{g}") for g in range(GROUPS)]
        keyed = sem("keyed")
        turned = sem("turned")
        by_edge_ready = sem("by_edge_ready")
        dve_step = sem("dve_step")
        hot_ready = sem("hot_ready")
        first_los_ready = sem("first_los_ready")
        distance_ready = sem("distance_ready")
        first_hot_ready = sem("first_hot_ready")
        window_done = sem("window_done")
        bank_free = sem("bank_free")
        stage_free = sem("stage_free")
        stage_seen = sem("stage_seen")
        loops_ready = sem("loops_ready")
        adj_placed = sem("adj_placed")
        adj_ready = sem("adj_ready")
        scalars_ready = sem("scalars_ready")

        pads_zeroed = sem("pads_zeroed")
        x_in = sem("x_in")
        weights_in = sem("weights_in")
        vec_turned = sem("vec_turned")
        abs_ready = sem("abs_ready")
        bound_ready = sem("bound_ready")
        diag_ready = sem("diag_ready")
        row_ready = sem("row_ready")
        centered = sem("centered")
        squared = sem("squared")
        h0_ready = sem("h0_ready")
        h0_squared = sem("h0_squared")
        scaled0 = sem("scaled0")
        hi0_ready = sem("hi0_ready")
        parts0_ready = sem("parts0_ready")
        h0_turned = sem("h0_turned")
        h0t_ready = sem("h0t_ready")
        kept_ready = sem("kept_ready")
        deg_ready = sem("deg_ready")
        dk_ready = sem("dk_ready")
        dk_turned = sem("dk_turned")
        dkrows_ready = sem("dkrows_ready")
        dk_out = sem("dk_out")
        db_in = sem("db_in")
        kb_in = sem("kb_in")
        agg_half = sem("agg_half")
        blocks_out = sem("blocks_out")
        agg_zeroed = sem("agg_zeroed")
        sq_ready = sem("sq_ready")
        norm_ready = sem("norm_ready")
        proj_ready = sem("proj_ready")
        proj_done = sem("proj_done")
        ss_ready = sem("ss_ready")
        h1_ready = sem("h1_ready")
        h1_squared = sem("h1_squared")
        rns_ready = sem("rns_ready")
        hi1_ready = sem("hi1_ready")
        lo1_ready = sem("lo1_ready")
        h1_turned = sem("h1_turned")
        h1t_ready = sem("h1t_ready")
        x_again = sem("x_again")
        h2_ready = sem("h2_ready")
        h2_turned = sem("h2_turned")
        h2t_ready = sem("h2t_ready")
        xt_ready = sem("xt_ready")
        xt_half = sem("xt_half")
        score_ready = sem("score_ready")
        totals_in = sem("totals_in")
        totals_out = sem("totals_out")
        hw_ready = sem("hw_ready")
        hw_kept = sem("hw_kept")
        hi_ready = sem("hi_ready")
        lo_ready = sem("lo_ready")
        v_centered = sem("v_centered")
        v_squared = sem("v_squared")
        coef_ready = sem("coef_ready")
        relu_done = sem("relu_done")
        xs_out = sem("xs_out")
        weights_fit = sem("weights_fit")
        xs_in = sem("xs_in")
        final_ready = sem("final_ready")
        final_turned = sem("final_turned")
        w2_ready = sem("w2_ready")
        stored = sem("stored")

        flag_sums_in = sem("flag_sums_in")
        flag_sums_out = sem("flag_sums_out")
        flag_ready = sem("flag_ready")
        tie_ready = sem("tie_ready")
        tie_step, tie_in, tie_out = ([sem(f"{n}{lv}") for lv in range(3)] for n in ("tie_step", "tie_in", "tie_out"))
        gen_const = sem("gen_const")
        gen_kept_ready = sem("gen_kept_ready")
        gen_table_out = sem("gen_table_out")
        gen_ids_in = sem("gen_ids_in")
        gen_rows_in = [sem(f"gen_rows_in{n}") for n in range(len(SUMS))]
        gen_ids_ready = sem("gen_ids_ready")
        gen_hot_ready = sem("gen_hot_ready")
        gen_used = sem("gen_used")
        gen_summed = sem("gen_summed")
        gen_degrees_back = sem("gen_degrees_back")

        block = ctx.enter_context(nc.Block())

        N_WEIGHTS = 15

        def chunk_keys(w):
            return [(0 if w >= LATE_WINDOWS % PER_IT else j0 * TILES, j1 * TILES) for j0, j1 in CHUNK_DESTS]

        def row_of(vector):
            return vector.rearrange("(o n) -> o n", o=1)

        def load_x(eng, signal):
            whole = (TILES - 1) * P
            eng.dma_start(nodebuf[:, 0:whole].rearrange("p (t f) -> p t f", f=FEAT),
                          a["x"][0:whole, :].rearrange("(t p) f -> p t f", p=P)).then_inc(signal, DMA)
            eng.dma_start(nodebuf[0:TAIL, whole:PAD], a["x"][whole:NODES, :]).then_inc(signal, DMA)

        @block.sync
        def _(sp):
            sp.dma_start(dst_in, a["dst"].rearrange("(p c) -> p c", p=EP)).then_inc(edges_in, DMA)
            sp.wait_ge(last_picked, 1)
            sp.dma_start(last_row.rearrange("(p c) -> p c", p=EP), last_in).then_inc(last_out, DMA)
            sp.wait_ge(last_out, DMA)
            sp.dma_start(last_all, last_row.rearrange("(o c) -> o c", o=1).broadcast_to((P, EDGES // GRAIN))).then_inc(last_back, DMA)
            for table, edges in ((src_table, a["src"]), (dst_table, a["dst"])):
                for r0, r1 in ((0, ROWS // 16 * 16), (ROWS // 16 * 16, ROWS)):
                    rows = bass.AP(edges.tensor, r0 * GRAIN, [[GRAIN, r1 - r0], [1, SLOTS]])
                    sp.dma_start(table[r0:r1, :], rows).then_inc(table_in, DMA)
            sp.wait_ge(parts0_ready, 1)
            sp.wait_ge(h0t_ready, len(GROUPS4))
            load_x(sp, x_again)
            loaded = 0
            for i, (kind, level, slot, slots, norm) in enumerate(CONVS):
                if i == 0 or i in POOLED:
                    sp.wait_ge(dkrows_ready, level + 1)
                    sp.dma_start(dk_dram[level], dk_rows).then_inc(dk_out, DMA)
                    sp.wait_ge(dk_out, DMA * (level + 1))
                if kind == "up":
                    sp.wait_ge(xs_out, DMA * 3)
                    sp.wait_ge(hw_ready, len(GROUPS4) * i)
                    sp.dma_start(skip_t, xs_dram[level]).then_inc(xs_in, DMA)
                row = dk_dram[level].rearrange("(v t) p -> v (t p)", v=2)
                if i == 0 or CONVS[i - 1][1] != level:
                    if i == 0:
                        sp.wait_ge(proj_done, 2 * TILES)
                    sp.wait_ge(blocks_out, BLOCKS * (FIRST_UNIT + i))
                    sp.dma_start(d_all, row[0:1, 0:COLS].broadcast_to((P, COLS))).then_inc(db_in, DMA)
                    if level > 0:
                        sp.wait_ge(xt_ready, i)
                        sp.dma_start(k_all, row[1:2, 0:COLS].broadcast_to((P, COLS))).then_inc(kb_in, DMA)
                if i in (1, 2, 3):
                    sp.wait_ge(xt_ready, i + 1)
                    sp.dma_start(xs_dram[level], nodes_t).then_inc(xs_out, DMA)
            sp.wait_ge(final_ready, len(GROUPS4))
            whole = (TILES - 1) * P
            sp.dma_start(out[0:whole, :].rearrange("(t p) f -> p t f", p=P),
                         nodebuf[:, 0:whole].rearrange("p (t f) -> p t f", f=FEAT)).then_inc(stored, DMA)
            sp.dma_start(out[whole:NODES, :], nodebuf[0:TAIL, whole:PAD]).then_inc(stored, DMA)
            sp.wait_ge(stored, 2 * DMA)

        @block.gpsimd
        def _(pool):
            pool.memset(ident[:], 0.0).then_inc(pool_step, 1)
            pool.wait_ge(pool_step, 1)
            pool.affine_select(out=ident[:], in_=ident[:], compare_op=ALU.not_equal, fill=1.0, base=0,
                               pattern=[[-1, P]], channel_multiplier=1).then_inc(consts_ready, 1)
            pool.iota(win_base[:], pattern=[[P * WIN, GROUPS]], base=0, channel_multiplier=WIN,
                      allow_small_or_imprecise_dtypes=True).then_inc(consts_ready, 1)
            pool.iota(iota_lo[:], pattern=[[1, P]], base=0, channel_multiplier=0,
                      allow_small_or_imprecise_dtypes=True).then_inc(consts_ready, 1)
            pool.iota(iota_key[:], pattern=[[1, KEYS]], base=0, channel_multiplier=0,
                      allow_small_or_imprecise_dtypes=True).then_inc(consts_ready, 1)
            pool.memset(ones[:], 1.0).then_inc(consts_ready, 1)
            for n, step in enumerate(WHOLE_STEPS):
                pool.iota(steps_iota[:, n, :], pattern=[[step, FAN]], base=-sum(WHOLE_STEPS[:n]), channel_multiplier=0,
                          allow_small_or_imprecise_dtypes=True).then_inc(consts_ready, 1)
            pool.iota(keys[:, 6, :], pattern=[[-P, TILES]], base=4095, channel_multiplier=-1,
                      allow_small_or_imprecise_dtypes=True).then_inc(consts_ready, 1)
            pool.memset(adj_words[:, :, COLS // 4:PAD // 4], 0).then_inc(adj_placed, 1)
            pool.wait_ge(rows_known, 1)
            pool.wait_ge(table_in, 4 * DMA)
            for g in range(GROUPS):
                for rows, table in ((edge_src, src_table), (edge_dst, dst_table)):
                    pool.indirect_dma_start(out=rows[:, g, :], out_offset=None, in_=table,
                                            in_offset=bass.IndirectOffsetOnAxis(ap=row_i[:, g:g + 1], axis=0)
                                            ).then_inc(gathered[g], DMA)
            pool.sem_inc(stage_free, 2)
            with pool.Fori(0, ITS) as it:
                for k in range(2):
                    pool.wait_ge(bank_free, it * PAIRS + (STAGE + STAGE * (k + 1)))
                    pool.tensor_copy(adj_words[:, :, bass.ds(it * (2 * PER_IT) + k * PER_IT, PER_IT)], stage_words[:, k]).then_inc(stage_free, 1)

            pool.wait_ge(flag_ready, 1)
            general = pool.value_load(flag[0:1, 0:1], min_val=0, max_val=1)
            with pool.If(general > 0):
                pool.iota(gen_cols, pattern=[[1, COLS]], base=0, channel_multiplier=0,
                          allow_small_or_imprecise_dtypes=True).then_inc(gen_const, 1)
                pool.iota(gen_nodes, pattern=[[P, TILES]], base=0, channel_multiplier=1,
                          allow_small_or_imprecise_dtypes=True).then_inc(gen_const, 1)
                pool.memset(gen_kept[:, :, P:2 * P], 0.0).then_inc(gen_const, 1)
                pool.wait_ge(gen_const, 3)
                for ids, edges in ((gen_all_src, a["src"]), (gen_all_dst, a["dst"])):
                    pool.dma_start(ids[0:EP, :], edges.rearrange("(p c) -> p c", p=EP)).then_inc(gen_ids_in, DMA)
                pool.wait_ge(gen_ids_in, 2 * DMA)
                tables = 0
                for n, (what, which) in enumerate(SUMS):
                    width = 512 if (what, which) in (("agg", 1), ("agg", 2)) else 256
                    table = gen_table[width]
                    view = table.rearrange("(t p) c -> p t c", p=P)
                    if n > 0:
                        pool.wait_ge(gen_used, n * GEN_STEPS)
                    if what == "deg":
                        pool.wait_ge(kept_ready, which + 1)
                        pool.tensor_copy(gen_kept[:, :, 0:P], per_node(kept16[:])).then_inc(gen_kept_ready, 1)
                        pool.wait_ge(gen_kept_ready, which + 1)
                        pool.dma_start(view, gen_kept).then_inc(gen_table_out, DMA)
                        tables += 1
                    elif which != 2:
                        if which == 0:
                            pool.wait_ge(parts0_ready, 1)
                        elif which == 1:
                            pool.wait_ge(lo1_ready, TILES)
                        else:
                            pool.wait_ge(lo_ready, TILES * (which - FIRST_UNIT + 1))
                        source = (parts1 if which == 1 else parts0).rearrange("p t k f -> p t (k f)")
                        pool.dma_start(view, source).then_inc(gen_table_out, DMA)
                        tables += 1
                    pool.wait_ge(gen_table_out, DMA * tables)

                    def self_loops(t):
                        pool.tensor_scalar(gen_hot, gen_cols, gen_nodes[:, t:t + 1], COUNT, ALU.is_equal, ALU.mult).then_inc(gen_hot_ready, 1)

                    self_loops(0)
                    with pool.Fori(0, EC) as c:
                        pool.wait_ge(gen_used, c + (n * GEN_STEPS + 1))
                        pool.wait_ge(flag_ready, 1)
                        pool.tensor_copy(gen_src[0:EP, :], gen_all_src[0:EP, bass.ds(c, 1)]).then_inc(gen_ids_ready, 1)
                        pool.tensor_copy(gen_dst_f[0:EP, :], gen_all_dst[0:EP, bass.ds(c, 1)]).then_inc(gen_ids_ready, 1)
                        pool.wait_ge(gen_ids_ready, c * 2 + (n * EC + 1) * 2)
                        pool.tensor_tensor(gen_spare[0:EP, :], gen_dst_f[0:EP, :], gen_dst_f[0:EP, :], ALU.add)
                        pool.indirect_dma_start(out=gen_rows[0:EP, 0:width], out_offset=None, in_=table,
                                                in_offset=bass.IndirectOffsetOnAxis(ap=gen_src[0:EP, :].bitcast(U32), axis=0)
                                                ).then_inc(gen_rows_in[n], DMA)
                        pool.tensor_scalar(gen_hot[0:EP, :], gen_cols[0:EP, :], gen_dst_f[0:EP, :], COUNT, ALU.is_equal, ALU.mult
                                           ).then_inc(gen_hot_ready, 1)
                    for t in range(1, TILES):
                        pool.wait_ge(gen_used, n * GEN_STEPS + EC + t)
                        self_loops(t)

        @block.vector
        def _(dve):
            steps = [0]

            def step(ins):
                ins.then_inc(dve_step, 1)
                steps[0] += 1
                dve.wait_ge(dve_step, steps[0])

            def rsqrt(to, of, half):
                v = nc.vector
                step(v.tensor_scalar(half.bitcast(I32), of.bitcast(I32), 1, None, ALU.logical_shift_right))
                step(v.tensor_scalar(to.bitcast(I32), half.bitcast(I32), -1.0, RSQRT_MAGIC, ALU.mult, ALU.add))
                for _ in range(3):
                    step(v.tensor_tensor(half, to, to, ALU.mult))
                    step(v.scalar_tensor_tensor(half, half, -0.5, of, ALU.mult, ALU.mult))
                    step(v.scalar_tensor_tensor(to, half, 1.5, to, ALU.add, ALU.mult))

            def inverse_norms(inv, norm, squares_sum):
                half = tiny[:, 11, :]
                step(nc.vector.tensor_scalar(norm, squares_sum, 1e-30, None, ALU.max))
                rsqrt(inv, norm, half)
                step(nc.vector.tensor_scalar(inv, inv, 1e12, None, ALU.min))
                step(nc.vector.tensor_tensor(norm, squares_sum, inv, ALU.mult))

            def layernorm(src, to, junk, n):
                total, inv = tiny[:, 0, :], tiny[:, 1, :]
                step(nc.vector.tensor_reduce(total, tiles(src), AX.X, ALU.add))
                step(nc.vector.tensor_scalar(total, total, -1.0 / FEAT, None, ALU.mult))
                nc.vector.tensor_tensor(tiles(src), tiles(src), per_node(total), ALU.add).then_inc(centered, 1)
                dve.wait_ge(centered, n)
                dve.wait_ge(squared, n)
                step(nc.vector.tensor_reduce(total, tiles(junk), AX.X, ALU.add))
                step(nc.vector.tensor_scalar(total, total, 1.0 / FEAT, 1e-5, ALU.mult, ALU.add))
                rsqrt(inv, total, tiny[:, 11, :])
                return nc.vector.scalar_tensor_tensor(tiles(to), tiles(src), 0.0, per_node(inv), ALU.max, ALU.mult)

            def fit_powers(c0, c1, psum_cols):
                bits = bn[:, 0:1] if c1 - c0 == 1 else tiny[:, 10, 0:c1 - c0]
                f, u = fit[:, c0:c1], unfit[:, c0:c1]
                step(nc.vector.tensor_scalar(bits, psum_cols, 2.0 ** -100, None, ALU.max))
                step(nc.vector.tensor_scalar(bits.bitcast(I32), bits.bitcast(I32), 0x7F800000, None, ALU.bitwise_and))
                step(nc.vector.tensor_scalar(f.bitcast(I32), bits.bitcast(I32), -1.0, float(268 << 23), ALU.mult, ALU.add))
                step(nc.vector.tensor_scalar(u.bitcast(I32), f.bitcast(I32), -1.0, float(254 + 3 << 23), ALU.mult, ALU.add))

            def fit_weights(i):
                _, _, slot, slots, _ = CONVS[i]
                fitted[0] += 1
                nc.vector.tensor_scalar(diag_fit, ident[:], fit[:, i:i + 1], None, ALU.mult).then_inc(diag_ready, 1)
                dve.wait_ge(row_ready, fitted[0] - len(fixed) + 1)
                w = weights[:, slot:slot + slots, :]
                row = psum[:, 7:8, 0:P].broadcast_to((P, slots, P))
                nc.vector.tensor_tensor(w, w, row, ALU.mult).then_inc(weights_fit, 1)
                dve.wait_ge(weights_fit, fitted[0])

            dve.wait_ge(edges_in, DMA)
            nc.vector.tensor_copy(last_in, dst_in.rearrange("p (c k) -> p c k", k=GRAIN)[:, :, GRAIN - 1]).then_inc(last_picked, 1)
            nc.vector.memset(nodebuf[:, PAD - P:PAD], 0.0).then_inc(pads_zeroed, 1)
            dve.wait_ge(consts_ready, 10)
            dve.wait_ge(last_back, DMA)
            for g in range(GROUPS):
                step(nc.vector.tensor_scalar(compared, last_all, win_base[:, g:g + 1], 0.0, ALU.is_lt, ALU.add,
                                             accum_out=row_f[:, g:g + 1]))
            nc.vector.tensor_scalar(row_i[:], row_f[:], float(ROWS - 1), None, ALU.min).then_inc(rows_known, 1)
            dve.wait_ge(x_in, 2 * DMA)
            layernorm(nodebuf[:], nodebuf[:], region3[:, 0:PAD], 1).then_inc(h0_ready, 1)
            dve.wait_ge(h0_squared, 1)
            step(nc.vector.tensor_reduce(tiny[:, 2, :], tiles(region3[:, 0:PAD]), AX.X, ALU.add))
            norm0 = tiny[:, 3, :]
            inverse_norms(tiny[:, 4, :], norm0, tiny[:, 2, :])
            step(nc.vector.tensor_scalar(tiny[:, 4, :], tiny[:, 4, :], UNIT_SCALE, None, ALU.mult))
            nc.vector.tensor_tensor(tiles(region3[:, PAD:2 * PAD]), tiles(nodebuf[:]), per_node(tiny[:, 4, :]), ALU.mult).then_inc(scaled0, 1)
            dve.wait_ge(hi0_ready, 1)
            nc.vector.tensor_tensor(parts0[:, :, 1, :], tiles(region3[:, PAD:2 * PAD]), parts0[:, :, 0, :], ALU.subtract).then_inc(parts0_ready, 1)
            dve.wait_ge(parts0_ready, 1)
            step(nc.vector.tensor_scalar(chunk2_dest[:], win_base[:], float(LATE_WINDOWS * WIN), float(CHUNK_DESTS[2][0]),
                                         ALU.is_lt, ALU.mult))
            for g in range(GROUPS):
                dve.wait_ge(gathered[g], 2 * DMA)
                low, high = work[0].bitcast(I32), work[1].bitcast(I32)
                late, outside = work[2], work[3]
                loc = key_rows[:, g, :]
                nc.vector.tensor_scalar(low, edge_src[:, g, :], P - 1, None, ALU.bitwise_and)
                nc.vector.tensor_scalar(high, edge_src[:, g, :], 7, None, ALU.logical_shift_right)
                step(nc.vector.tensor_scalar(loc, edge_dst[:, g, :], win_base[:, g:g + 1], None, ALU.subtract))
                nc.vector.tensor_copy(lo_rows[:, g, :], low)
                nc.vector.tensor_scalar(late[:, 0:P], loc[:, 0:P], float(CHUNK_DESTS[0][1]), None, ALU.is_ge)
                step(nc.vector.tensor_scalar(late[:, P:SLOTS], loc[:, P:SLOTS], float(WIN), None, ALU.is_ge))
                for n, (s0, s1, first_dest) in enumerate(((0, 2 * P, 0.0), (2 * P, SLOTS, chunk2_dest[:, g:g + 1]))):
                    step(nc.vector.scalar_tensor_tensor(outside[:, s0:s1], loc[:, s0:s1], first_dest, late[:, s0:s1],
                                                        ALU.is_lt, ALU.max, accum_out=uncovered[:, 2 * g + n:2 * g + n + 1]))
                step(nc.vector.scalar_tensor_tensor(loc, loc, float(TILES), high, ALU.mult, ALU.add))
                nc.vector.scalar_tensor_tensor(loc, outside, 4096.0, loc, ALU.mult, ALU.add).then_inc(keyed, 1)
            dve.wait_ge(by_edge_ready, 2 * GROUPS)
            nc.vector.memset(seen, 0).then_inc(stage_seen, 1)
            nc.vector.memset(stage_words[:, 1], 0).then_inc(stage_seen, 1)
            nc.vector.tensor_scalar(loops, ident[:], COUNT, None, ALU.mult).then_inc(loops_ready, 1)
            dve.sem_inc(hot_ready, 1)

            def see(k, stages_before, stages_out):
                dve.wait_ge(stage_seen, stages_before + 2)
                dve.wait_ge(bank_free, stages_out * STAGE + STAGE)
                nc.vector.tensor_tensor(seen, seen, stage_words[:, k], ALU.bitwise_or).then_inc(stage_seen, 1)

            with dve.Fori(0, ITS) as it:
                dve.wait_ge(hot_ready, it * PER_IT + 1)
                nc.vector.tensor_copy(scalars[:], by_edge[:, :, bass.ds(PER_IT * it, PER_IT), :]).then_inc(scalars_ready, 1)
                dve.wait_ge(scalars_ready, it + 1)
                for w in range(0, PER_IT, 2):
                    dve.wait_ge(window_done, it * PER_IT + (w + 2))
                    r = w % RING
                    nc.vector.tensor_tensor(hot_lo[:, r:r + 2, 1:CHUNKS, :],
                                            iota_lo[:].rearrange("p (o q n) -> p o q n", o=1, q=1).broadcast_to((P, 2, CHUNKS - 1, P)),
                                            scalars[:, 0, w:w + 2, 1:CHUNKS].rearrange("p w (c o) -> p w c o", o=1).broadcast_to((P, 2, CHUNKS - 1, P)),
                                            ALU.is_equal)
                    if w == 6:
                        see(1, it * 2, it * 2)
                    if w == 20:
                        see(0, it * 2 + 1, it * 2 + 1)
                    k0, k1 = chunk_keys(w)[2]
                    nc.vector.tensor_tensor(hot_key2[:, r:r + 2, k0:k1],
                                            iota_key[:, k0:k1].rearrange("p (o n) -> p o n", o=1).broadcast_to((P, 2, k1 - k0)),
                                            scalars[:, 1, w:w + 2, 2:3].broadcast_to((P, 2, k1 - k0)), ALU.is_equal)
                    for v in (w, w + 1):
                        for c, (k0, k1) in enumerate(chunk_keys(v)[0:2]):
                            last = nc.vector.tensor_scalar(hot_key[:, v % RING, c, k0:k1], iota_key[:, k0:k1],
                                                           scalars[:, 1, v, c:c + 1], None, ALU.is_equal)
                        last.then_inc(hot_ready, 1)

            see(1, 2 * ITS, 2 * ITS)
            dve.wait_ge(loops_ready, 1)
            dve.wait_ge(stage_free, 2 + 2 * ITS)
            for t in range(0, TILES, TILES - 1):
                n = TILES - 1 if t == 0 else 1
                o = t * (PAD + P)
                if t == 0:
                    diag = adj[:, 0:n * (PAD + P)].rearrange("p (t n) -> p t n", t=n)[:, :, 0:P]
                    one = loops.rearrange("p (o n) -> p o n", o=1).broadcast_to((P, n, P))
                else:
                    diag, one = adj[:, o:o + P], loops
                nc.vector.tensor_tensor(diag, diag, one, ALU.add, saturate=False).then_inc(adj_ready, 1)

            def degrees(level):
                with dve.If(general > 0):
                    dve.wait_ge(gen_summed, level + 1)
                    if level > 0:
                        dve.wait_ge(deg_ready, level)
                    nc.vector.memset(gen_degrees[:, COLS:PAD], 1.0).then_inc(gen_degrees_back, 1)
                    for b in range(BLOCKS):
                        nc.vector.tensor_copy(gen_degrees[:, b * BLOCK:(b + 1) * BLOCK], psum[:, b, 0:BLOCK]).then_inc(gen_degrees_back, 1)
                    dve.wait_ge(gen_degrees_back, (BLOCKS + 1) * (level + 1))
                dve.wait_ge(deg_ready, level + 1)
                d, kept, half, deg = dcol[:, level, 0, :], dcol[:, level, 1, :], tiny[:, 11, :], tiny[:, 10, :]
                step(nc.vector.tensor_scalar(deg, psum[:, 7, 0:TILES], 1.0 / COUNT, 1.0, ALU.mult, ALU.max))
                rsqrt(d, deg, half)
                nc.vector.tensor_tensor(d, d, kept, ALU.mult).then_inc(dk_ready, 1)
                dve.wait_ge(dk_ready, level + 1)
                dve.wait_ge(dk_turned, level + 1)
                if level > 0:
                    dve.wait_ge(dk_out, DMA * level)
                nc.vector.tensor_copy(dk_rows, psum[0:2 * TILES, 7, P:2 * P]).then_inc(dkrows_ready, 1)
                dve.wait_ge(dkrows_ready, level + 1)

            def blocks_of(unit, b0, b1, take):
                for b in range(b0, b1):
                    if b in (0, 4):
                        dve.wait_ge(agg_half, 2 * unit + (1 if b == 0 else 2))
                    take(b).then_inc(blocks_out, 1)

            def first_agg(to):
                return lambda b: nc.vector.tensor_scalar(to[:, b * BLOCK:(b + 1) * BLOCK], psum[:, b, 0:BLOCK],
                                                         1.0 / (UNIT_SCALE * COUNT), None, ALU.mult)

            def project(layer, width, bias, factor, to):
                for t in range(TILES):
                    m = layer * TILES + t
                    dve.wait_ge(proj_ready, m + 1)
                    tmp = proj_tmp[:, t % 2, 0:width]
                    step(nc.vector.tensor_tensor(tmp, psum[:, t % 4, 256:256 + width], bias[:], ALU.add))
                    nc.vector.scalar_tensor_tensor(to[:, t, :], psum[:, t % 4, 0:width], factor[:, t:t + 1], tmp,
                                                   ALU.mult, ALU.add).then_inc(proj_done, 1)
                    if layer == 0 and t > 0:
                        positive_squares(t - 1)
                if layer == 0:
                    positive_squares(TILES - 1)

            def positive_squares(t):
                dve.wait_ge(proj_done, t + 1)
                nc.vector.scalar_tensor_tensor(junk1[:, t, :], out0[:, t, :], 0.0, out0[:, t, :], ALU.max, ALU.mult,
                                               accum_out=tiny[:, 9, t:t + 1]).then_inc(h1_squared, 1)

            def agg_factor(layer, norm):
                dve.wait_ge(norm_ready, layer + 1)
                factor, other, total = tiny[:, 5, :], tiny[:, 6, :], tiny[:, 7, :]
                step(nc.vector.tensor_copy(total, psum[:, 7, 0:TILES]))
                inverse_norms(factor, other, total)
                step(nc.vector.tensor_scalar(factor, factor, scales[:, layer:layer + 1], None, ALU.mult))
                step(nc.vector.tensor_tensor(factor, factor, norm, ALU.mult))
                return factor

            dve.wait_ge(adj_ready, 2)
            step(nc.vector.tensor_reduce(search[:, 16:17], uncovered[:], AX.X, ALU.add))
            dve.wait_ge(stage_seen, 2 * ITS + 3)
            step(nc.vector.tensor_scalar(seen, seen, FULL, None, ALU.bitwise_and))
            nc.vector.tensor_reduce(search[:, 17:18], seen.bitcast(I32), AX.XY, ALU.max).then_inc(flag_sums_in, 1)
            dve.wait_ge(flag_sums_out, 1)
            step(nc.vector.tensor_scalar(search[:, 18:19], psum[:, 7, 480:481], float(GROUPS * P * SLOTS - EDGES), None, ALU.not_equal))
            step(nc.vector.tensor_scalar(search[:, 19:20], psum[:, 7, 481:482], 0.0, None, ALU.is_gt))
            nc.vector.tensor_tensor(flag[:], search[:, 18:19], search[:, 19:20], ALU.max).then_inc(flag_ready, 1)
            dve.wait_ge(flag_ready, 1)
            general = dve.value_load(flag[0:1, 0:1], min_val=0, max_val=1)
            step(nc.vector.memset(dcol[:, 0, 1, :], 1.0))
            step(nc.vector.memset(dcol[:, 0, 1, TILES - 1:TILES], 0.0))
            step(nc.vector.memset(dcol[0:TAIL, 0, 1, TILES - 1:TILES], 1.0))
            nc.vector.tensor_copy(kept16[:], dcol[:, 0, 1, :]).then_inc(kept_ready, 1)
            dve.wait_ge(kept_ready, 1)
            nc.vector.memset(agg0t[:, COLS:PAD], 0.0).then_inc(agg_zeroed, 1)
            dve.wait_ge(vec_turned, 1)
            step(nc.vector.tensor_copy(vecs[:], psum[:, 7, 0:V_ROWS]))
            step(nc.vector.tensor_tensor(search[:, 0:3], vecs[:, V_POOL:V_POOL + 3], vecs[:, V_POOL:V_POOL + 3], ALU.mult))
            magnitude = search[:, 16:16 + V_ROWS]
            step(nc.vector.tensor_scalar(magnitude.bitcast(I32), vecs[:].bitcast(I32), 0x7FFFFFFF, None, ALU.bitwise_and))
            step(nc.vector.memset(bounds[:], 1.0))
            step(nc.vector.memset(bounds[:, 0:1], 11.4))
            for slot, g, beta in [(2 + k, V_DN_G + k, V_DN_BETA + k) for k in range(3)] + \
                                 [(6 + 2 * k, V_DN_G + 2 - k, V_DN_BETA + 2 - k) for k in range(3)] + \
                                 [(7 + 2 * k, V_UP_G + k, V_UP_BETA + k) for k in range(2)] + [(11, V_UP_G + 2, V_UP_BETA + 2)]:
                step(nc.vector.scalar_tensor_tensor(bounds[:, slot:slot + 1], magnitude[:, g:g + 1], 56.0, magnitude[:, beta:beta + 1],
                                                    ALU.mult, ALU.add))
            dve.wait_ge(weights_in, N_WEIGHTS * DMA)
            nc.vector.tensor_scalar(abs_w.bitcast(I32), weights[:].bitcast(I32), 0x7FFFFFFF, None, ALU.bitwise_and).then_inc(abs_ready, 1)
            blocks_of(0, 0, 4, first_agg(agg0t))
            dve.wait_ge(bound_ready, 1)
            step(nc.vector.tensor_scalar(pool_norm[:], psum[:, 7, 32:35], 1e-30, None, ALU.max))
            step(nc.vector.tensor_copy(search[:, 4:7], pool_norm[:]))
            rsqrt(pool_norm[:], search[:, 4:7], search[:, 8:11])
            fit_powers(0, 9, psum[:, 7, 16:25])
            fixed = [i for i in range(len(CONVS)) if i not in UNSCALED]
            for n, i in enumerate(fixed):
                nc.vector.tensor_scalar(diag_fits[:, n, :], ident[:], fit[:, i:i + 1], None, ALU.mult).then_inc(diag_ready, 1)
            blocks_of(0, 4, BLOCKS, first_agg(agg0t))
            dve.wait_ge(row_ready, 1)
            for n, i in enumerate(fixed):
                _, _, slot, slots, _ = CONVS[i]
                w = weights[:, slot:slot + slots, :]
                row = psum[:, n // 4:n // 4 + 1, n % 4 * P:(n % 4 + 1) * P].broadcast_to((P, slots, P))
                nc.vector.tensor_tensor(w, w, row, ALU.mult).then_inc(weights_fit, 1)
            fitted = [len(fixed)]
            dve.wait_ge(w2_ready, 8 * DMA)
            factor = agg_factor(0, norm0)
            project(0, 256, bias0, factor, out0)
            dve.wait_ge(ss_ready, 1)
            inverse_norms(tiny[:, 5, :], tiny[:, 6, :], tiny[:, 8, :])
            dve.wait_ge(h1_squared, TILES)
            norm1 = tiny[:, 3, :]
            for _ in range(2):
                step(nc.vector.tensor_tensor(tiny[:, 9, :], tiny[:, 9, :], tiny[:, 5, :], ALU.mult))
            inverse_norms(tiny[:, 4, :], norm1, tiny[:, 9, :])
            nc.vector.tensor_scalar(tiny[:, 4, :], tiny[:, 4, :], UNIT_SCALE, None, ALU.mult).then_inc(rns_ready, 1)
            dve.wait_ge(rns_ready, 1)
            for g in range(len(GROUPS2) + 2):
                if g < len(GROUPS2):
                    t0, n = GROUPS2[g]
                    inv = tiny[:, 5, t0:t0 + n].rearrange("p (t o) -> p t o", o=1).broadcast_to((P, n, 256))
                    nc.vector.scalar_tensor_tensor(out0[:, t0:t0 + n, :], out0[:, t0:t0 + n, :], 0.0, inv, ALU.max, ALU.mult
                                                   ).then_inc(h1_ready, 1)
                if g >= 2:
                    t0, n = GROUPS2[g - 2]
                    for t in range(t0, t0 + n):
                        dve.wait_ge(h1_ready, g - 1)
                        dve.wait_ge(hi1_ready, t + 1)
                        nc.vector.scalar_tensor_tensor(parts1[:, t, 1, :], out0[:, t, :], tiny[:, 4, t:t + 1], parts1[:, t, 0, :],
                                                       ALU.mult, ALU.subtract).then_inc(lo1_ready, 1)
            dve.wait_ge(h1t_ready, len(GROUPS2))
            dve.wait_ge(lo1_ready, TILES)
            for m in range(2):
                nc.vector.memset(agg1t[:, m, COLS:PAD], 0.0).then_inc(agg_zeroed, 1)
            for m in range(2):
                blocks_of(1 + m, 0, BLOCKS, first_agg(agg1t[:, m, :]))
            factor = agg_factor(1, norm1)
            project(1, P, bias1, factor, tiles(out1))
            dve.wait_ge(ss_ready, 2)
            inverse_norms(tiny[:, 5, :], tiny[:, 6, :], tiny[:, 8, :])
            step(nc.vector.tensor_tensor(tiles(out1), tiles(out1), per_node(tiny[:, 5, :]), ALU.mult))
            dve.wait_ge(x_again, 2 * DMA)
            step(nc.vector.tensor_tensor(nodebuf[:], nodebuf[:], out1, ALU.add))
            step(nc.vector.tensor_copy(out1, nodebuf[:]))
            layernorm(out1, out1, region1[:, 0:PAD], 2).then_inc(h2_ready, 1)
            dve.wait_ge(h2_ready, 1)
            degrees(0)
            dve.wait_ge(h2t_ready, len(GROUPS4))

            vec = lambda k: vecs[:, k:k + 1]
            totals = [0]

            def tanh(to, x, p, x2):
                v = nc.vector
                step(v.tensor_scalar(x, x, TANH_CLAMP, -TANH_CLAMP, ALU.min, ALU.max))
                step(v.tensor_tensor(x2, x, x, ALU.mult))
                step(v.tensor_scalar(p, x2, TANH_P[0], None, ALU.mult))
                for c in TANH_P[1:-1]:
                    step(v.scalar_tensor_tensor(p, p, c, x2, ALU.add, ALU.mult))
                step(v.scalar_tensor_tensor(p, p, TANH_P[-1], x, ALU.add, ALU.mult))
                step(v.tensor_scalar(to, x2, TANH_Q[0], None, ALU.mult))
                for c in TANH_Q[1:-1]:
                    step(v.scalar_tensor_tensor(to, to, c, x2, ALU.add, ALU.mult))
                step(v.tensor_scalar(to, to, TANH_Q[-1], None, ALU.add))
                step(v.reciprocal(x2, to))
                step(v.tensor_tensor(to, p, x2, ALU.mult))
                step(v.tensor_scalar(to, to, BELOW_1, -BELOW_1, ALU.min, ALU.max))
                step(v.tensor_scalar(p, x, TANH_CLAMP, 1.0 - BELOW_1, ALU.is_ge, ALU.mult))
                step(v.tensor_tensor(to, to, p, ALU.add))
                step(v.tensor_scalar(p, x, -TANH_CLAMP, 1.0 - BELOW_1, ALU.is_le, ALU.mult))
                step(v.tensor_tensor(to, to, p, ALU.subtract))

            def choose(level):
                v = nc.vector
                kept, chosen = dcol[:, level, 1, :], dcol[:, level + 1, 1, :]
                x, p, x2, th = (tiny[:, k, :] for k in range(5, 9))
                dve.wait_ge(score_ready, level + 1)
                step(v.tensor_scalar(x, psum[:, 7, 0:TILES], pool_norm[:, level:level + 1], None, ALU.mult))
                tanh(th, x, p, x2)
                step(v.tensor_scalar(th, th, 0.0, None, ALU.add))
                sign, bits = p.bitcast(I32), th.bitcast(I32)
                step(v.tensor_scalar(sign, bits, 31, 0x7FFFFFFF, ALU.arith_shift_right, ALU.bitwise_and))
                step(v.tensor_tensor(bits, bits, sign, ALU.bitwise_xor))
                step(v.tensor_scalar(sign, bits, 16, None, ALU.arith_shift_right))
                step(v.tensor_scalar(keys[:, 2 * level, :], sign, 32769.0, None, ALU.add))
                step(v.tensor_scalar(sign, bits, 0xFFFF, None, ALU.bitwise_and))
                step(v.tensor_scalar(keys[:, 2 * level + 1, :], sign, 1.0, None, ALU.add))
                equal, key, above = key_work[:, 0, :], key_work[:, 1, :], key_work[:, 2, :]
                base, need, count = search[:, 0:1], search[:, 1:2], search[:, 2:3]
                step(v.tensor_copy(equal, kept))
                step(v.memset(chosen, 0.0))
                step(v.memset(need, float(LEVEL_NODES[level + 1])))

                def narrow(which, steps, step, total):
                    step(v.tensor_tensor(key, keys[:, which, :], equal, ALU.mult))
                    skipped = len(WHOLE_STEPS) - len(steps)
                    step(v.memset(base, 1.0 + sum(WHOLE_STEPS[:skipped])))
                    for n, size in enumerate(steps):
                        step(v.scalar_tensor_tensor(
                            compare_buf, key.rearrange("p (o t) -> p o t", o=1).broadcast_to((P, FAN, TILES)), base,
                            steps_iota[:, skipped + n, :].rearrange("p (j o) -> p j o", o=1).broadcast_to((P, FAN, TILES)),
                            ALU.subtract, ALU.is_ge))
                        total(v.tensor_reduce(search[:, 16:16 + FAN], compare_buf, AX.X, ALU.add))
                        step(v.tensor_scalar(search[:, 48:48 + FAN], psum[:, 7, 0:FAN], need, 0.0, ALU.is_ge, ALU.add, accum_out=count))
                        step(v.scalar_tensor_tensor(base, count, float(size), base, ALU.mult, ALU.add))
                    step(v.tensor_scalar(base, base, -float(sum(WHOLE_STEPS)), None, ALU.add))
                    step(v.tensor_scalar(above, key, base, 0.0, ALU.is_gt, ALU.add, accum_out=search[:, 16:17]))
                    total(v.tensor_scalar(equal, key, base, 0.0, ALU.is_equal, ALU.add, accum_out=search[:, 17:18]))
                    step(v.tensor_tensor(chosen, chosen, above, ALU.add))
                    step(v.tensor_tensor(need, need, psum[:, 7, 0:1], ALU.subtract))

                def total(ins):
                    ins.then_inc(totals_in, 1)
                    totals[0] += 1
                    dve.wait_ge(totals_out, totals[0])

                for which, steps in score_keys(level):
                    narrow(which, steps, step, total)
                v.tensor_tensor(tie[:], psum[:, 7, 1:2], need, ALU.is_gt).then_inc(tie_ready, 1)
                dve.wait_ge(tie_ready, level + 1)
                tied = dve.value_load(tie[0:1, 0:1], min_val=0, max_val=1)
                with dve.If(tied > 0):
                    tie_counts = [0, 0]

                    def tie_link(ins):
                        ins.then_inc(tie_step[level], 1)
                        tie_counts[0] += 1
                        dve.wait_ge(tie_step[level], tie_counts[0])

                    def tie_total(ins):
                        ins.then_inc(tie_in[level], 1)
                        tie_counts[1] += 1
                        dve.wait_ge(tie_out[level], tie_counts[1])

                    for which, steps in tie_keys(level):
                        narrow(which, steps, tie_link, tie_total)
                step(v.tensor_tensor(chosen, chosen, equal, ALU.add))
                v.tensor_copy(kept16[:], chosen).then_inc(kept_ready, 1)
                dve.wait_ge(kept_ready, level + 2)

            spread = [0, 0]
            for i, (kind, level, slot, slots, norm) in enumerate(CONVS):
                unit, v = FIRST_UNIT + i, nc.vector
                if i in POOLED:
                    choose(level - 1)
                    degrees(level)
                if i in UNSCALED:
                    step(v.tensor_reduce(bounds[:, slot:slot + 1], nodes_t, AX.X, ALU.max, apply_absolute_value=True))
                    v.tensor_scalar(abs_w.bitcast(I32), weights[:].bitcast(I32), 0x7FFFFFFF, None, ALU.bitwise_and).then_inc(abs_ready, 1)
                    dve.wait_ge(bound_ready, 2 + UNSCALED.index(i))
                    fit_powers(i, i + 1, psum[:, 7, 16 + i:17 + i])
                    fit_weights(i)
                for t in range(TILES if i in POOLED else 0):
                    dve.wait_ge(hi_ready, TILES * i + t + 1)
                    v.scalar_tensor_tensor(parts0[:, t, 1, :], agg_t[:, t * P:(t + 1) * P], dcol[:, level, 0, t:t + 1],
                                           parts0[:, t, 0, :], ALU.mult, ALU.subtract).then_inc(lo_ready, 1)
                for t in range(TILES if i not in POOLED else 0):
                    dve.wait_ge(hi_ready, TILES * i + min(t - t % 4 + 4, TILES))
                    v.scalar_tensor_tensor(parts0[:, t, 1, :], psum[:, 4 + t // 4 % 4, (t % 4) * P:(t % 4 + 1) * P],
                                           dcol[:, level, 0, t:t + 1], parts0[:, t, 0, :], ALU.mult, ALU.subtract
                                           ).then_inc(lo_ready, 1)
                if i == 0 or CONVS[i - 1][1] != level:
                    spread[0] += 1
                    dve.wait_ge(db_in, DMA * spread[0])
                    if level > 0:
                        spread[1] += 1
                        dve.wait_ge(kb_in, DMA * spread[1])
                if i in POOLED:
                    dve.wait_ge(lo_ready, TILES * (i + 1))
                blocks_of(unit, 0, BLOCKS, lambda b: v.scalar_tensor_tensor(
                    agg_t[:, b * BLOCK:(b + 1) * BLOCK], psum[:, b, 0:BLOCK], unfit[:, i:i + 1], d_all[:, b * BLOCK:(b + 1) * BLOCK],
                    ALU.mult, ALU.mult, accum_out=block_sums[:, b:b + 1]))
                dve.wait_ge(blocks_out, BLOCKS * (unit + 1))
                real = agg_t[:, 0:NODES] if level == 0 else agg_t[:, 0:COLS]
                kept = k_all
                if norm is None:
                    bias = vec({"in": V_IN_B, "bot": V_BOT_B, "out": V_OUT_B}[kind])
                    if kind == "in":
                        step(v.tensor_scalar(nodes_t[:, 0:COLS], agg_t[:, 0:COLS], bias, None, ALU.add))
                    elif kind == "bot":
                        step(v.tensor_scalar(agg_t[:, 0:COLS], agg_t[:, 0:COLS], bias, 0.0, ALU.add, ALU.max))
                        dve.wait_ge(xs_out, DMA * 3)
                        step(v.tensor_tensor(nodes_t[:, 0:COLS], agg_t[:, 0:COLS], kept, ALU.mult))
                    else:
                        step(v.tensor_scalar(agg_t[:, 0:COLS], agg_t[:, 0:COLS], bias, None, ALU.add))
                else:
                    g, beta, bias = ((V_DN_G, V_DN_BETA, V_DN_B) if kind == "dn" else (V_UP_G, V_UP_BETA, V_UP_B))
                    total, minus_mean, inv, gain, half, sq0, sq1 = (bn[:, k:k + 1] for k in range(7))
                    step(v.tensor_reduce(total, block_sums[:], AX.X, ALU.add))
                    step(v.tensor_scalar(total, total, 1.0 / LEVEL_NODES[level], vec(bias + norm), ALU.mult, ALU.add))
                    step(v.tensor_scalar(minus_mean, total, -1.0, vec(bias + norm), ALU.mult, ALU.add))
                    for c0, c1 in halves(level):
                        if level == 0:
                            v.tensor_scalar(agg_t[:, c0:c1], agg_t[:, c0:c1], minus_mean, None, ALU.add).then_inc(v_centered, 1)
                        else:
                            v.scalar_tensor_tensor(agg_t[:, c0:c1], agg_t[:, c0:c1], minus_mean, kept[:, c0:c1],
                                                   ALU.add, ALU.mult).then_inc(v_centered, 1)
                    normed = sum(c[4] is not None for c in CONVS[:i]) + 1
                    dve.wait_ge(v_squared, 2 * normed)
                    step(v.tensor_tensor(sq0, sq0, sq1, ALU.add))
                    step(v.tensor_scalar(inv, sq0, 1.0 / LEVEL_NODES[level], 1e-5, ALU.mult, ALU.add))
                    rsqrt(gain, inv, half)
                    v.tensor_tensor(gain, gain, vec(g + norm), ALU.mult).then_inc(coef_ready, 1)
                    for h, (c0, c1) in enumerate(halves(level)):
                        dve.wait_ge(relu_done, 2 * normed - 1 + h)
                        if kind == "up" and level > 0:
                            step(v.tensor_tensor(nodes_t[:, c0:c1], nodes_t[:, c0:c1], kept[:, c0:c1], ALU.mult))
                        if h == 0:
                            v.memset(spare[:], 0.0).then_inc(xt_half, 1)
                            dve.wait_ge(xt_half, normed)
                if kind != "out":
                    v.memset(nodes_t[:, COLS:PAD], 0.0).then_inc(xt_ready, 1)
                    dve.wait_ge(xt_ready, i + 1)
                else:
                    v.memset(agg_t[:, COLS:PAD], 0.0).then_inc(xt_ready, 1)
            for g, (t0, n) in enumerate(GROUPS4):
                dve.wait_ge(final_turned, g + 1)
                nc.vector.tensor_tensor(nodebuf[:, t0 * P:(t0 + n) * P], nodebuf[:, t0 * P:(t0 + n) * P],
                                        psum[:, g, 0:n * P], ALU.add).then_inc(final_ready, 1)

        @block.scalar
        def _(act):
            act.wait_ge(pads_zeroed, 1)
            load_x(act, x_in)
            act.dma_start(vec_rows[V_IN_B:V_IN_B + 1, :], row_of(a["L1_gnn_in_b"])).then_inc(weights_in, DMA)
            for row, name in ((V_DN_B, "dn_b"), (V_DN_G, "dn_g"), (V_DN_BETA, "dn_beta"), (V_POOL, "pool_w"),
                              (V_UP_B, "up_b"), (V_UP_G, "up_g"), (V_UP_BETA, "up_beta")):
                act.dma_start(vec_rows[row:row + 3, :], a["L1_gnn_" + name]).then_inc(weights_in, DMA)
            act.dma_start(vec_rows[V_BOT_B:V_BOT_B + 1, :], row_of(a["L1_gnn_bot_b"])).then_inc(weights_in, DMA)
            act.dma_start(vec_rows[V_OUT_B:V_OUT_B + 1, :], row_of(a["L1_gnn_out_b"])).then_inc(weights_in, DMA)
            act.dma_start(weights[:, 0, :], a["L1_gnn_in_W"]).then_inc(weights_in, DMA)
            act.dma_start(weights[:, 1:4, :], a["L1_gnn_dn_W"].rearrange("s k f -> k s f")).then_inc(weights_in, DMA)
            act.dma_start(weights[:, 4, :], a["L1_gnn_bot_W"]).then_inc(weights_in, DMA)
            act.dma_start(weights[:, 5:11, :], a["L1_gnn_up_W"].rearrange("s (h k) f -> k (s h) f", h=2)).then_inc(weights_in, DMA)
            act.dma_start(weights[:, 11, :], a["L1_gnn_out_W"]).then_inc(weights_in, DMA)
            act.wait_ge(centered, 1)
            nc.scalar.activation(region3[:, 0:PAD], nodebuf[:], ACT.Square).then_inc(squared, 1)
            act.wait_ge(h0_ready, 1)
            nc.scalar.activation(region3[:, 0:PAD], nodebuf[:], ACT.Square).then_inc(h0_squared, 1)
            act.wait_ge(scaled0, 1)
            nc.scalar.activation(parts0[:, :, 0, :], tiles(region3[:, PAD:2 * PAD]), ACT.Copy).then_inc(hi0_ready, 1)
            act.wait_ge(parts0_ready, 1)
            act.dma_start(wl0[:], a["L0_gnn_Wl0"]).then_inc(w2_ready, DMA)
            act.dma_start(wr0[:], a["L0_gnn_Wr0"]).then_inc(w2_ready, DMA)
            act.dma_start(wl1[:], a["L0_gnn_Wl1"].rearrange("(m k) f -> k m f", m=2)).then_inc(w2_ready, DMA)
            act.dma_start(wr1[:], a["L0_gnn_Wr1"].rearrange("(m k) f -> k m f", m=2)).then_inc(w2_ready, DMA)
            act.dma_start(bias0[:], row_of(a["L0_gnn_bl0"]).broadcast_to((P, 256))).then_inc(w2_ready, DMA)
            act.dma_start(bias1[:], row_of(a["L0_gnn_bl1"]).broadcast_to((P, P))).then_inc(w2_ready, DMA)
            act.dma_start(scales[:, 0:1], row_of(a["L0_gnn_scale0"]).broadcast_to((P, 1))).then_inc(w2_ready, DMA)
            act.dma_start(scales[:, 1:2], row_of(a["L0_gnn_scale1"]).broadcast_to((P, 1))).then_inc(w2_ready, DMA)
            for g in range(GROUPS):
                for k in range(2):
                    act.wait_ge(turned, 2 * g + k + 1)
                    nc.scalar.activation(by_edge[:, k, g * P:(g + 1) * P, :],
                                         psum[:, 2 * (g % 2) + k, 0:CHUNKS * P].rearrange("p (c w) -> p w c", c=CHUNKS),
                                         ACT.Copy).then_inc(by_edge_ready, 1)
            for g, (t0, n) in enumerate(GROUPS4):
                act.wait_ge(h0_turned, g + 1)
                nc.scalar.activation(h0t[:, t0 * P:(t0 + n) * P], psum[:, g % 4, 0:n * P], ACT.Copy).then_inc(h0t_ready, 1)
            act.sem_inc(bank_free, STAGE)
            act.wait_ge(consts_ready, 10)

            def first_chunks(b, done):
                w = 2 * b
                act.wait_ge(first_hot_ready, done)
                for v in range(2):
                    last = nc.scalar.activation(lo_distance[:, v], iota_lo[:], ACT.Abs, bias=first_los[:, w + v], scale=-1.0)
                last.then_inc(distance_ready, 1)

                def second_step():
                    act.wait_ge(window_done, done * 2 + 2)
                    act.wait_ge(distance_ready, done + 1)
                    nc.scalar.activation(hot_lo[:, w % RING:w % RING + 2, 0, :], lo_distance, ACT.Relu, bias=ones[:, 0:1], scale=-1.0
                                         ).then_inc(first_hot_ready, 1)
                return second_step

            nc.scalar.activation(first_los, by_edge[:, 0, 0:PER_IT, 0:1], ACT.Copy).then_inc(first_los_ready, 1)
            act.wait_ge(first_los_ready, 1)
            for v in range(2):
                last = nc.scalar.activation(lo_distance[:, v], iota_lo[:], ACT.Abs, bias=first_los[:, v], scale=-1.0)
            last.then_inc(distance_ready, 1)
            act.wait_ge(distance_ready, 1)
            nc.scalar.activation(hot_lo[:, 0:2, 0, :], lo_distance, ACT.Relu, bias=ones[:, 0:1], scale=-1.0).then_inc(first_hot_ready, 1)
            with act.Fori(0, ITS) as it:
                for b in range(PAIRS):
                    if b == PAIRS - 1:
                        act.wait_ge(distance_ready, it * PAIRS + PAIRS)
                        nc.scalar.activation(first_los, by_edge[:, 0, bass.ds(it * PER_IT + PER_IT, PER_IT), 0:1], ACT.Copy).then_inc(first_los_ready, 1)
                        act.wait_ge(first_los_ready, it + 2)
                    next_hot = first_chunks((b + 1) % PAIRS, it * PAIRS + (b + 1))
                    act.wait_ge(window_done, it * PER_IT + (RING + 2 * b + 2))
                    if b % STAGE == 0:
                        act.wait_ge(stage_free, 2 * it + (b // STAGE + 1))
                        act.wait_ge(stage_seen, 2 * it + (b // STAGE + 2))
                    act.wait_ge(bank_free, it * PAIRS + (b + 1))
                    next_hot()
                    at = 2 * WIN * (b % STAGE)
                    nc.scalar.activation(stage[:, b // STAGE, :, at:at + 2 * WIN],
                                         psum[:, b % STAGE, 0:2 * KEYS].rearrange("p (j t) -> p t j", t=TILES),
                                         ACT.Copy, scale=COUNT, saturate=False).then_inc(bank_free, 1)

            act.wait_ge(blocks_out, BLOCKS)
            act.wait_ge(agg_zeroed, 1)
            nc.scalar.activation(squares, agg0t, ACT.Square).then_inc(sq_ready, 1)
            for t in range(TILES):
                act.wait_ge(proj_done, t + 1)
                last = nc.scalar.activation(junk0[:, t, :], out0[:, t, :], ACT.Square, accum_out=tiny[:, 8, t:t + 1])
            last.then_inc(ss_ready, 1)
            act.wait_ge(rns_ready, 1)
            for t in range(TILES):
                act.wait_ge(h1_ready, t // 2 + 1)
                nc.scalar.activation(parts1[:, t, 0, :], out0[:, t, :], ACT.Copy, scale=tiny[:, 4, t:t + 1]).then_inc(hi1_ready, 1)
                if t % 2 or t == TILES - 1:
                    g = t // 2
                    t0, n = GROUPS2[g]
                    act.wait_ge(h1_turned, g + 1)
                    nc.scalar.activation(h1t[:, :, t0 * P:(t0 + n) * P],
                                         psum[:, g % 4, 0:2 * n * P].rearrange("p (m n) -> p m n", m=2), ACT.Copy).then_inc(h1t_ready, 1)
            act.wait_ge(blocks_out, 3 * BLOCKS)
            act.wait_ge(agg_zeroed, 3)
            nc.scalar.activation(squares1, agg1t, ACT.Square).then_inc(sq_ready, 1)
            act.wait_ge(norm_ready, 2)
            for t in range(TILES):
                act.wait_ge(proj_done, TILES + t + 1)
                last = nc.scalar.activation(junk2[:, t, :], tiles(out1)[:, t, :], ACT.Square, accum_out=tiny[:, 8, t:t + 1])
            last.then_inc(ss_ready, 1)
            act.wait_ge(centered, 2)
            nc.scalar.activation(region1[:, 0:PAD], out1, ACT.Square).then_inc(squared, 1)
            for g, (t0, n) in enumerate(GROUPS4):
                act.wait_ge(h2_turned, g + 1)
                nc.scalar.activation(nodes_t[:, t0 * P:(t0 + n) * P], psum[:, g % 4, 0:n * P], ACT.Copy).then_inc(h2t_ready, 1)
            normed = 0
            for i, (kind, level, slot, slots, norm) in enumerate(CONVS):
                if i in POOLED:
                    for g, (t0, n) in enumerate(GROUPS4):
                        act.wait_ge(hw_ready, len(GROUPS4) * i + g + 1)
                        nc.scalar.activation(agg_t[:, t0 * P:(t0 + n) * P], psum[:, g, 0:n * P], ACT.Copy).then_inc(hw_kept, 1)
                    act.wait_ge(hw_kept, len(GROUPS4) * (POOLED.index(i) + 1))
                    act.wait_ge(dk_ready, level + 1)
                    for t in range(TILES):
                        nc.scalar.activation(parts0[:, t, 0, :], agg_t[:, t * P:(t + 1) * P], ACT.Copy,
                                             scale=dcol[:, level, 0, t:t + 1]).then_inc(hi_ready, 1)
                for t in range(TILES if i not in POOLED else 0):
                    act.wait_ge(hw_ready, len(GROUPS4) * i + t // 4 + 1)
                    nc.scalar.activation(parts0[:, t, 0, :], psum[:, 4 + t // 4 % 4, (t % 4) * P:(t % 4 + 1) * P], ACT.Copy,
                                         scale=dcol[:, level, 0, t:t + 1]).then_inc(hi_ready, 1)
                if norm is not None:
                    normed += 1
                    for h, (c0, c1) in enumerate(halves(level)):
                        act.wait_ge(v_centered, 2 * normed - 1 + h)
                        nc.scalar.activation(squares[:, c0:c1], agg_t[:, c0:c1], ACT.Square, accum_out=bn[:, 5 + h:6 + h]).then_inc(v_squared, 1)
                    act.wait_ge(coef_ready, normed)
                    if kind == "dn" and level > 0:
                        act.wait_ge(xs_out, DMA * level)
                    beta = (V_DN_BETA if kind == "dn" else V_UP_BETA) + norm
                    for h, (c0, c1) in enumerate(halves(level)):
                        nc.scalar.activation(nodes_t[:, c0:c1], agg_t[:, c0:c1], ACT.Relu, bias=vecs[:, beta:beta + 1],
                                             scale=bn[:, 3:4]).then_inc(relu_done, 1)

        def input_bound(pe, i):
            _, _, slot, slots, _ = CONVS[i]
            for k in range(slots):
                last = pe.matmul(psum[:, 7, 16 + i:17 + i], abs_w[:, slot + k, :], bounds[:, slot + k:slot + k + 1],
                                 start=(k == 0), stop=(k == slots - 1))
            return last

        def fit_row(pe, n):
            pe.wait_ge(diag_ready, n + 1)
            pe.matmul(psum[:, 7, 0:P], ones[:], diag_fit, start=True, stop=True).then_inc(row_ready, 1)

        @block.tensor
        def _(pe):
            pe.wait_ge(consts_ready, 10)
            for g in range(GROUPS):
                pe.wait_ge(keyed, g + 1)
                for k, rows in enumerate((lo_rows, key_rows)):
                    if g >= 2:
                        pe.wait_ge(by_edge_ready, 2 * (g - 2) + k + 1)
                    for c in range(CHUNKS):
                        last = pe.transpose(psum[:, 2 * (g % 2) + k, c * P:(c + 1) * P], rows[:, g, c * P:(c + 1) * P], ident[:])
                    last.then_inc(turned, 1)
            for g, (t0, n) in enumerate(GROUPS4):
                pe.wait_ge(by_edge_ready, 2 * GROUPS)
                if g >= 4:
                    pe.wait_ge(h0t_ready, g - 3)
                for t in range(t0, t0 + n):
                    last = pe.transpose(psum[:, g % 4, (t - t0) * P:(t - t0 + 1) * P], nodebuf[:, t * P:(t + 1) * P], ident[:])
                last.then_inc(h0_turned, 1)
            pe.wait_ge(h0t_ready, len(GROUPS4))
            pe.sem_inc(window_done, RING)
            with pe.Fori(0, ITS) as it:
                for w in range(PER_IT):
                    pe.wait_ge(hot_ready, it * PER_IT + (w + 2))
                    b = w // 2 % STAGE
                    if w % 2 == 0:
                        pe.wait_ge(bank_free, it * PAIRS + (w // 2 + 1))
                        pe.wait_ge(first_hot_ready, it * PAIRS + (w // 2 + 1))
                    for n, c in enumerate((1, 0, 2)):
                        k0, k1 = chunk_keys(w)[c]
                        at = w % 2 * KEYS
                        last = pe.matmul(psum[:, b, at + k0:at + k1], hot_lo[:, w % RING, c, :],
                                         hot_key[:, w % RING, c, k0:k1] if c < 2 else hot_key2[:, w % RING, k0:k1], start=(n == 0), stop=(n == CHUNKS - 1))
                    last.then_inc(window_done, 1)

            def general_sum(n, weight, rows):
                first = n * GEN_STEPS

                def products(lhs, k_rows, begin, end):
                    for k in range(len(lhs)):
                        for b in range(BLOCKS):
                            last = pe.matmul(psum[:, b, 0:BLOCK], lhs[k], gen_hot[0:k_rows, b * BLOCK:(b + 1) * BLOCK],
                                             start=begin and k == 0, stop=end and k == len(lhs) - 1)
                    last.then_inc(gen_used, 1)
                    return last

                pe.wait_ge(gen_hot_ready, first + 1)
                products(weight(0), P, True, False)
                with pe.Fori(0, EC) as c:
                    pe.wait_ge(gen_hot_ready, c + (first + 2))
                    pe.wait_ge(gen_rows_in[n], c * DMA + DMA)
                    products(rows, EP, False, False)
                for t in range(1, TILES):
                    pe.wait_ge(gen_hot_ready, first + 1 + EC + t)
                    products(weight(t), P, False, t == TILES - 1)

            def aggregate(unit, weight, ready, first, products=None, waited=None):
                with pe.If(general > 0):
                    before = waited and waited[0]
                    for g in range(3, len(GROUPS4) if products else 0):
                        products(g)
                    if waited:
                        waited[0] = before
                    pe.wait_ge(blocks_out, BLOCKS * unit) if unit > 0 else None
                    if ready is not None:
                        pe.wait_ge(ready, first + TILES - 1)
                    m = P if unit == 2 else 0
                    width = 256 if unit in (1, 2) else P
                    general_sum(SUMS.index(("agg", unit)), lambda t: [weight(t, k) for k in range(2)],
                                [gen_rows[0:EP, k * width + m:k * width + m + P] for k in range(2)])
                    pe.wait_ge(gen_used, (SUMS.index(("agg", unit)) + 1) * GEN_STEPS)
                    pe.sem_inc(agg_half, 2)
                with pe.Else():
                    fast_aggregate(unit, weight, ready, first, products)

            def bound_all():
                pe.wait_ge(abs_ready, 1)
                pe.matmul(psum[:, 7, 32:35], ones[:], search[:, 0:3], start=True, stop=True)
                for i in range(len(CONVS)):
                    bound = input_bound(pe, i)
                bound.then_inc(bound_ready, 1)

            def fast_aggregate(unit, weight, ready, first, products):
                for half, (b0, b1) in enumerate(((0, 4), (4, BLOCKS))):
                    if unit > 0:
                        pe.wait_ge(blocks_out, BLOCKS * (unit - 1) + (4 if half == 0 else BLOCKS))
                    for t in range(TILES):
                        if half == 0 and ready is not None:
                            pe.wait_ge(ready, first + t)
                            if products and t % 4 == 1 and t // 4 + 3 < len(GROUPS4):
                                products(t // 4 + 3)
                        for k in range(2):
                            for b in range(b0, b1):
                                last = pe.matmul(psum[:, b, 0:BLOCK], weight(t, k),
                                                 adj[:, t * PAD + b * BLOCK:t * PAD + (b + 1) * BLOCK],
                                                 start=(t == 0 and k == 0), stop=(t == TILES - 1 and k == 1))
                    last.then_inc(agg_half, 1)

            def row_norms(pairs):
                for t in range(TILES):
                    for m, sq in enumerate(pairs):
                        last = pe.matmul(psum[:, 7, t:t + 1], sq[:, t * P:(t + 1) * P], ones[:, 0:1],
                                         start=(m == 0), stop=(m == len(pairs) - 1))
                last.then_inc(norm_ready, 1)

            def project(layer, sums, rows, wl, wr, width):
                for t in range(TILES):
                    m = layer * TILES + t
                    if t >= 4:
                        pe.wait_ge(proj_done, m - 3)
                    for col, lhs, w in ((0, sums, wl), (256, rows, wr)):
                        for k in range(len(lhs)):
                            last = pe.matmul(psum[:, t % 4, col:col + width], lhs[k][:, t * P:(t + 1) * P], w[k],
                                             start=(k == 0), stop=(k == len(lhs) - 1))
                    last.then_inc(proj_ready, 1)

            def degree_sums(level):
                pe.wait_ge(kept_ready, level + 1)
                with pe.If(general > 0):
                    if level == 0:
                        pe.wait_ge(proj_done, 2 * TILES)
                    else:
                        pe.wait_ge(hw_kept, len(GROUPS4) * level)
                    pe.wait_ge(gen_kept_ready, level + 1)
                    n = SUMS.index(("deg", level))
                    general_sum(n, lambda t: [gen_kept[:, t, 0:P]], [gen_rows[0:EP, 0:P]])
                    pe.wait_ge(gen_used, (n + 1) * GEN_STEPS)
                    pe.sem_inc(gen_summed, 1)
                    pe.wait_ge(gen_degrees_back, (BLOCKS + 1) * (level + 1))
                    for t in range(TILES):
                        last = pe.matmul(psum[:, 7, t:t + 1], gen_degrees[0:1, t * P:(t + 1) * P], ones[0:1, 0:1], start=True, stop=True)
                    last.then_inc(deg_ready, 1)
                with pe.Else():
                    for d in range(TILES):
                        for t in range(TILES):
                            last = pe.matmul(psum[:, 7, d:d + 1], adj[:, t * PAD + d * P:t * PAD + (d + 1) * P], kept16[:, t:t + 1],
                                             start=(t == 0), stop=(t == TILES - 1))
                    last.then_inc(deg_ready, 1)

            def turn_degrees(level):
                pe.wait_ge(dk_ready, level + 1)
                pe.transpose(psum[0:2 * TILES, 7, P:2 * P], dcol[:, level].rearrange("p v t -> p (v t)"), ident[:]).then_inc(dk_turned, 1)

            pe.wait_ge(weights_in, N_WEIGHTS * DMA)
            pe.transpose(psum[:, 7, 0:V_ROWS], vec_rows[:], ident[0:V_ROWS, 0:V_ROWS]).then_inc(vec_turned, 1)
            pe.wait_ge(flag_sums_in, 1)
            pe.matmul(psum[:, 7, 480:482], ones[:], search[:, 16:18], start=True, stop=True).then_inc(flag_sums_out, 1)
            pe.wait_ge(flag_ready, 1)
            general = pe.value_load(flag[0:1, 0:1], min_val=0, max_val=1)
            pe.wait_ge(adj_ready, 2)
            pe.wait_ge(parts0_ready, 1)
            bound_all()
            aggregate(0, lambda t, k: parts0[:, t, k, :], None, 0)
            fixed = len(CONVS) - len(UNSCALED)
            pe.wait_ge(blocks_out, 4)
            pe.wait_ge(diag_ready, fixed)
            for n in range(fixed):
                last = pe.matmul(psum[:, n // 4, n % 4 * P:(n % 4 + 1) * P], ones[:], diag_fits[:, n, :], start=True, stop=True)
            last.then_inc(row_ready, 1)
            pe.wait_ge(sq_ready, 1)
            row_norms([squares])
            pe.wait_ge(blocks_out, BLOCKS)
            pe.wait_ge(w2_ready, 8 * DMA)
            pe.wait_ge(weights_fit, fixed)
            project(0, [agg0t], [h0t], [wl0[:]], [wr0[:]], 256)
            for g, (t0, n) in enumerate(GROUPS2):
                if g >= 4:
                    pe.wait_ge(h1t_ready, g - 3)
                pe.wait_ge(h1_ready, g + 1)
                for m in range(2):
                    for t in range(t0, t0 + n):
                        last = pe.transpose(psum[:, g % 4, (m * n + t - t0) * P:(m * n + t - t0 + 1) * P],
                                            out0[:, t, m * P:(m + 1) * P], ident[:])
                last.then_inc(h1_turned, 1)
            pe.wait_ge(h1t_ready, len(GROUPS2))
            for m in range(2):
                aggregate(1 + m, lambda t, k: parts1[:, t, k, m * P:(m + 1) * P], lo1_ready if m == 0 else None, 1)
            pe.wait_ge(sq_ready, 2)
            row_norms([squares1[:, 0, :], squares1[:, 1, :]])
            project(1, [agg1t[:, 0, :], agg1t[:, 1, :]], [h1t[:, 0, :], h1t[:, 1, :]],
                    [wl1[:, 0, :], wl1[:, 1, :]], [wr1[:, 0, :], wr1[:, 1, :]], P)
            degree_sums(0)
            pe.wait_ge(h2_ready, 1)
            for g, (t0, n) in enumerate(GROUPS4):
                if g >= 4:
                    pe.wait_ge(h2t_ready, g - 3)
                for t in range(t0, t0 + n):
                    last = pe.transpose(psum[:, g % 4, (t - t0) * P:(t - t0 + 1) * P], out1[:, t * P:(t + 1) * P], ident[:])
                last.then_inc(h2_turned, 1)
            turn_degrees(0)

            totals = 0
            up = 0
            for i, (kind, level, slot, slots, norm) in enumerate(CONVS):
                if i == 0:
                    pe.wait_ge(h2t_ready, len(GROUPS4))
                elif CONVS[i - 1][4] is None:
                    pe.wait_ge(xt_ready, i)
                else:
                    pe.wait_ge(xt_half, sum(c[4] is not None for c in CONVS[:i]))
                rest = i > 0 and CONVS[i - 1][4] is not None
                if i in POOLED:
                    for t in range(TILES):
                        if t * P == HALF:
                            pe.wait_ge(xt_ready, i)
                            rest = False
                        last = pe.matmul(psum[:, 7, t:t + 1], nodes_t[:, t * P:(t + 1) * P], vecs[:, V_POOL + level - 1:V_POOL + level],
                                         start=True, stop=True)
                    last.then_inc(score_ready, 1)
                    rounds = [n for _, steps in score_keys(level - 1) for n in [FAN] * len(steps) + [2]]
                    for r, n in enumerate(rounds):
                        totals += 1
                        pe.wait_ge(totals_in, totals)
                        pe.matmul(psum[:, 7, 0:n], ones[:], search[:, 16:16 + n], start=True, stop=True).then_inc(totals_out, 1)
                        if 1 <= r <= len(GROUPS4):
                            g = r - 1
                            t0, m = GROUPS4[g]
                            for t in range(t0, t0 + m):
                                last = pe.matmul(psum[:, g, (t - t0) * P:(t - t0 + 1) * P], nodes_t[:, t * P:(t + 1) * P],
                                                 weights[:, slot, :], start=True, stop=True)
                            last.then_inc(hw_ready, 1)
                    pe.wait_ge(tie_ready, level)
                    tied = pe.value_load(tie[0:1, 0:1], min_val=0, max_val=1)
                    with pe.If(tied > 0):
                        rounds = [n for _, steps in tie_keys(level - 1) for n in [FAN] * len(steps) + [2]]
                        for r, n in enumerate(rounds):
                            pe.wait_ge(tie_in[level - 1], r + 1)
                            pe.matmul(psum[:, 7, 0:n], ones[:], search[:, 16:16 + n], start=True, stop=True).then_inc(tie_out[level - 1], 1)
                    degree_sums(level)
                    turn_degrees(level)
                if i in UNSCALED:
                    n = UNSCALED.index(i)
                    pe.wait_ge(abs_ready, 2 + n)
                    input_bound(pe, i).then_inc(bound_ready, 1)
                    fit_row(pe, len(CONVS) - len(UNSCALED) + n)
                pe.wait_ge(dkrows_ready, max(c[1] for c in CONVS[:i + 1]) + 1)
                if kind == "up":
                    up += 1
                    pe.wait_ge(xs_in, DMA * up)
                pe.wait_ge(weights_fit, len(CONVS) - len(UNSCALED) + sum(u <= i for u in UNSCALED))
                inputs = [nodes_t, skip_t][:slots]
                waited = [not rest]

                def products(g):
                    t0, n = GROUPS4[g]
                    if g >= 4:
                        pe.wait_ge(lo_ready, TILES * i + 4 * (g - 3))
                    for t in range(t0, t0 + n):
                        if t * P == HALF and not waited[0]:
                            pe.wait_ge(xt_ready, i)
                            waited[0] = True
                        for k, x in enumerate(inputs):
                            last = pe.matmul(psum[:, 4 + g % 4, (t - t0) * P:(t - t0 + 1) * P], x[:, t * P:(t + 1) * P],
                                             weights[:, slot + k, :], start=(k == 0), stop=(k == slots - 1))
                    last.then_inc(hw_ready, 1)

                if i not in POOLED:
                    for g in range(3):
                        products(g)
                aggregate(FIRST_UNIT + i, lambda t, k: parts0[:, t, k, :], lo_ready, TILES * i + 1,
                          None if i in POOLED else products, waited)
            pe.wait_ge(xt_ready, len(CONVS))
            for g, (t0, n) in enumerate(GROUPS4):
                for t in range(t0, t0 + n):
                    last = pe.transpose(psum[:, g, (t - t0) * P:(t - t0 + 1) * P], agg_t[:, t * P:(t + 1) * P], ident[:])
                last.then_inc(final_turned, 1)


_INS = ["x", "src", "dst", "L0_gnn_Wl0", "L0_gnn_bl0", "L0_gnn_Wr0", "L0_gnn_Wl1", "L0_gnn_bl1", "L0_gnn_Wr1",
        "L0_gnn_scale0", "L0_gnn_scale1", "L1_gnn_in_W", "L1_gnn_in_b", "L1_gnn_dn_W", "L1_gnn_dn_b", "L1_gnn_dn_g",
        "L1_gnn_dn_beta", "L1_gnn_pool_w", "L1_gnn_bot_W", "L1_gnn_bot_b", "L1_gnn_up_W", "L1_gnn_up_b", "L1_gnn_up_g",
        "L1_gnn_up_beta", "L1_gnn_out_W", "L1_gnn_out_b"]


def kernel(**inputs):
    import numpy as np
    import concourse.bacc as bacc
    from concourse.bass_utils import run_bass_kernel_spmd

    nc = bacc.Bacc("TRN2", target_bir_lowering=False, num_devices=1)
    arrays, args = {}, {}
    for name in _INS:
        x = np.ascontiguousarray(inputs[name]).reshape(inputs[name].shape or (1,))
        arrays["in_" + name] = x
        args[name] = nc.dram_tensor("in_" + name, x.shape, mybir.dt.from_np(x.dtype), kind="ExternalInput").ap()
    out = nc.dram_tensor("out", (NODES, FEAT), F32, kind="ExternalOutput").ap()
    gnn_kernel(nc, args, out)
    return run_bass_kernel_spmd(nc, [arrays], core_ids=[0]).results[0]["out"]
```
